# Optimizing a Trainium2 kernel written in Bass

```python
import numpy as np
import jax
import jax.numpy as jnp

def _softmax(x, axis=-1):
    return jax.nn.softmax(x, axis=axis)
def _gelu(x):
    return jax.nn.gelu(x, approximate=True)
def _silu(x):
    return jax.nn.silu(x)
def _sigmoid(x):
    return jax.nn.sigmoid(x)
def _layernorm(x, axis=-1, eps=1e-5):
    m = jnp.mean(x, axis=axis, keepdims=True)
    v = jnp.var(x, axis=axis, keepdims=True)
    return (x - m) / jnp.sqrt(v + eps)
def _scatter_add(tgt, idx, src, axis=0):
    return tgt.at[idx].add(src)
def _segment_sum(src, seg, n):
    return jax.ops.segment_sum(src, seg, n)

kernel_name = 'mk_conv_seq_d1_conv_nchw128_0a5bc7'

def setup_inputs(seed: int = 0):
    np.random.seed(seed)
    _w = jnp.asarray
    def _rec_inputs():
        import jax
        import jax.numpy as jnp
        _gk = jax.random.key(seed)
        x = -0.0002928 + 1 * jax.random.normal(jax.random.fold_in(_gk, 1), (8, 128, 64, 64), jnp.float32)
        return x
    x = _rec_inputs()
    def _L0_conv_setup():
        import jax, jax.numpy as jnp
        import numpy as np
        from jax import lax
        B, C, H, W = (8, 128, 64, 64)
        DS, HD = (64, 32)
        DIN = 2 * C
        NH = DIN // HD
        DCONV = 4
        CONVCH = DIN + 2 * DS
        NBR = 5
        GN_GROUPS = 8
        TEMP = 10000.0

        def _perms():
            idx = np.arange(H * W).reshape(H, W)
            row = idx.reshape(-1)
            col = idx.T.reshape(-1)
            sh = idx.copy()
            sh[1::2] = sh[1::2, ::-1]
            sv = idx.T.copy()
            sv[1::2] = sv[1::2, ::-1]
            perms = [row, col, sh.reshape(-1), sv.reshape(-1)]
            return ([jnp.asarray(p) for p in perms], [jnp.asarray(np.argsort(p)) for p in perms])
        PERMS, INVS = _perms()

        def _pos_emb():
            half = C // 2
            dim_t = TEMP ** (np.arange(0, half, 2, dtype=np.float32) / half)
            ph = np.arange(H, dtype=np.float32)[:, None] / dim_t
            pw = np.arange(W, dtype=np.float32)[:, None] / dim_t
            eh = np.stack([np.sin(ph), np.cos(ph)], 2).reshape(H, -1)[:, :half]
            ew = np.stack([np.sin(pw), np.cos(pw)], 2).reshape(W, -1)[:, :C - half]
            emb = np.concatenate([np.broadcast_to(eh[:, None, :], (H, W, half)), np.broadcast_to(ew[None, :, :], (H, W, C - half))], -1)
            return jnp.asarray(emb.transpose(2, 0, 1))
        POS = _pos_emb()

        def _mamba(u, Wi, cw, Alog, dtb, Dp, nw, Wo):
            b, L, _ = u.shape
            zxbcdt = u @ Wi
            z = zxbcdt[..., :DIN]
            xBC = zxbcdt[..., DIN:DIN + CONVCH]
            dt = zxbcdt[..., DIN + CONVCH:]
            xBC = lax.conv_general_dilated(xBC, cw[:, None, :], (1,), [(DCONV - 1, 0)], dimension_numbers=('NWC', 'WIO', 'NWC'), feature_group_count=CONVCH)
            xBC = jax.nn.silu(xBC)
            xh = xBC[..., :DIN].reshape(b, L, NH, HD)
            Bm = xBC[..., DIN:DIN + DS]
            Cm = xBC[..., DIN + DS:]
            dt = jax.nn.softplus(dt + dtb)
            dA = jnp.exp(dt * -jnp.exp(Alog))

            def step(h, inp):
                dA_t, dt_t, x_t, B_t, C_t = inp
                h = dA_t[:, :, None, None] * h + (dt_t[:, :, None] * x_t)[..., None] * B_t[:, None, None, :]
                y = jnp.einsum('bhdn,bn->bhd', h, C_t)
                return (h, y)
            xs = (dA.transpose(1, 0, 2), dt.transpose(1, 0, 2), xh.transpose(1, 0, 2, 3), Bm.transpose(1, 0, 2), Cm.transpose(1, 0, 2))
            h0 = jnp.zeros((b, NH, HD, DS), u.dtype)
            _, ys = lax.scan(step, h0, xs)
            y = ys.transpose(1, 0, 2, 3) + Dp[None, None, :, None] * xh
            y = y.reshape(b, L, DIN) * jax.nn.silu(z)
            y = y * lax.rsqrt(jnp.mean(y * y, -1, keepdims=True) + 1e-05) * nw
            return y @ Wo

        def _forward(x, pos_proj_w, local_w, W_in, conv_w, A_log, dt_bias, Dp, norm_w, W_out, se_w1, se_b1, se_w2, se_b2, proj_w, gn_gamma, gn_beta):
            xp = x + jnp.einsum('chw,oc->ohw', POS.astype(x.dtype), pos_proj_w)[None]
            local = jax.nn.gelu(lax.conv_general_dilated(xp, local_w, (1, 1), 'SAME', dimension_numbers=('NCHW', 'OIHW', 'NCHW'), feature_group_count=C))
            seq = xp.reshape(B, C, H * W).transpose(0, 2, 1)
            branches = [local]
            for i in range(4):
                u = jnp.take(seq, PERMS[i], axis=1)
                y = _mamba(u, W_in[i], conv_w[i], A_log[i], dt_bias[i], Dp[i], norm_w[i], W_out[i])
                y = jnp.take(y, INVS[i], axis=1)
                branches.append(y.transpose(0, 2, 1).reshape(B, C, H, W))
            stacked = jnp.stack(branches, 1)
            desc = stacked.mean(axis=(2, 3, 4))
            wts = jax.nn.sigmoid(jax.nn.gelu(desc @ se_w1 + se_b1) @ se_w2 + se_b2)
            fused = (stacked * wts[:, :, None, None, None]).sum(1)
            concat = stacked.reshape(B, NBR * C, H, W)
            proj = jnp.einsum('bihw,oi->bohw', concat, proj_w)
            g = proj.reshape(B, GN_GROUPS, -1)
            g = (g - g.mean(-1, keepdims=True)) * lax.rsqrt(g.var(-1, keepdims=True) + 1e-05)
            proj = jax.nn.gelu(g.reshape(B, C, H, W) * gn_gamma[None, :, None, None] + gn_beta[None, :, None, None])
            return x + fused + proj
        key = jax.random.key(seed)
        ks = jax.random.split(key, 20)
        n = lambda k, s, sc: jax.random.normal(k, s, jnp.float32) * sc
        return {'x': n(ks[0], (B, C, H, W), 1.0), 'pos_proj_w': n(ks[1], (C, C), C ** (-0.5)), 'local_w': n(ks[2], (C, 1, 3, 3), 0.2), 'W_in': n(ks[3], (4, C, DIN + CONVCH + NH), C ** (-0.5)), 'conv_w': n(ks[4], (4, DCONV, CONVCH), 0.3), 'A_log': n(ks[5], (4, NH), 0.5), 'dt_bias': n(ks[6], (4, NH), 0.5), 'Dp': n(ks[7], (4, NH), 1.0), 'norm_w': jnp.ones((4, DIN), jnp.float32) + n(ks[8], (4, DIN), 0.02), 'W_out': n(ks[9], (4, DIN, C), DIN ** (-0.5)), 'se_w1': n(ks[10], (NBR, 2), 0.5), 'se_b1': n(ks[11], (2,), 0.1), 'se_w2': n(ks[12], (2, NBR), 0.5), 'se_b2': n(ks[13], (NBR,), 0.1), 'proj_w': n(ks[14], (C, NBR * C), (NBR * C) ** (-0.5)), 'gn_gamma': jnp.ones((C,), jnp.float32), 'gn_beta': jnp.zeros((C,), jnp.float32)}
    _L0_conv_all = _L0_conv_setup()
    _L0_conv_in = {k: v for k, v in _L0_conv_all.items() if k in ('pos_proj_w', 'local_w', 'W_in', 'conv_w', 'A_log', 'dt_bias', 'Dp', 'norm_w', 'W_out', 'se_w1', 'se_b1', 'se_w2', 'se_b2', 'proj_w', 'gn_gamma', 'gn_beta', )}
    del _L0_conv_all

    return {
        "x": x,
        "L0_conv_pos_proj_w": _L0_conv_in["pos_proj_w"],
        "L0_conv_local_w": _L0_conv_in["local_w"],
        "L0_conv_W_in": _L0_conv_in["W_in"],
        "L0_conv_conv_w": _L0_conv_in["conv_w"],
        "L0_conv_A_log": _L0_conv_in["A_log"],
        "L0_conv_dt_bias": _L0_conv_in["dt_bias"],
        "L0_conv_Dp": _L0_conv_in["Dp"],
        "L0_conv_norm_w": _L0_conv_in["norm_w"],
        "L0_conv_W_out": _L0_conv_in["W_out"],
        "L0_conv_se_w1": _L0_conv_in["se_w1"],
        "L0_conv_se_b1": _L0_conv_in["se_b1"],
        "L0_conv_se_w2": _L0_conv_in["se_w2"],
        "L0_conv_se_b2": _L0_conv_in["se_b2"],
        "L0_conv_proj_w": _L0_conv_in["proj_w"],
        "L0_conv_gn_gamma": _L0_conv_in["gn_gamma"],
        "L0_conv_gn_beta": _L0_conv_in["gn_beta"],
    }

def reference(x, L0_conv_pos_proj_w, L0_conv_local_w, L0_conv_W_in, L0_conv_conv_w, L0_conv_A_log, L0_conv_dt_bias, L0_conv_Dp, L0_conv_norm_w, L0_conv_W_out, L0_conv_se_w1, L0_conv_se_b1, L0_conv_se_w2, L0_conv_se_b2, L0_conv_proj_w, L0_conv_gn_gamma, L0_conv_gn_beta):
    import jax
    import jax.numpy as jnp
    def _L0_conv_ref(x, pos_proj_w, local_w, W_in, conv_w, A_log, dt_bias, Dp, norm_w, W_out, se_w1, se_b1, se_w2, se_b2, proj_w, gn_gamma, gn_beta):
        import jax, jax.numpy as jnp
        import numpy as np
        from jax import lax
        B, C, H, W = (8, 128, 64, 64)
        DS, HD = (64, 32)
        DIN = 2 * C
        NH = DIN // HD
        DCONV = 4
        CONVCH = DIN + 2 * DS
        NBR = 5
        GN_GROUPS = 8
        TEMP = 10000.0

        def _perms():
            idx = np.arange(H * W).reshape(H, W)
            row = idx.reshape(-1)
            col = idx.T.reshape(-1)
            sh = idx.copy()
            sh[1::2] = sh[1::2, ::-1]
            sv = idx.T.copy()
            sv[1::2] = sv[1::2, ::-1]
            perms = [row, col, sh.reshape(-1), sv.reshape(-1)]
            return ([jnp.asarray(p) for p in perms], [jnp.asarray(np.argsort(p)) for p in perms])
        PERMS, INVS = _perms()

        def _pos_emb():
            half = C // 2
            dim_t = TEMP ** (np.arange(0, half, 2, dtype=np.float32) / half)
            ph = np.arange(H, dtype=np.float32)[:, None] / dim_t
            pw = np.arange(W, dtype=np.float32)[:, None] / dim_t
            eh = np.stack([np.sin(ph), np.cos(ph)], 2).reshape(H, -1)[:, :half]
            ew = np.stack([np.sin(pw), np.cos(pw)], 2).reshape(W, -1)[:, :C - half]
            emb = np.concatenate([np.broadcast_to(eh[:, None, :], (H, W, half)), np.broadcast_to(ew[None, :, :], (H, W, C - half))], -1)
            return jnp.asarray(emb.transpose(2, 0, 1))
        POS = _pos_emb()

        def _mamba(u, Wi, cw, Alog, dtb, Dp, nw, Wo):
            b, L, _ = u.shape
            zxbcdt = u @ Wi
            z = zxbcdt[..., :DIN]
            xBC = zxbcdt[..., DIN:DIN + CONVCH]
            dt = zxbcdt[..., DIN + CONVCH:]
            xBC = lax.conv_general_dilated(xBC, cw[:, None, :], (1,), [(DCONV - 1, 0)], dimension_numbers=('NWC', 'WIO', 'NWC'), feature_group_count=CONVCH)
            xBC = jax.nn.silu(xBC)
            xh = xBC[..., :DIN].reshape(b, L, NH, HD)
            Bm = xBC[..., DIN:DIN + DS]
            Cm = xBC[..., DIN + DS:]
            dt = jax.nn.softplus(dt + dtb)
            dA = jnp.exp(dt * -jnp.exp(Alog))

            def step(h, inp):
                dA_t, dt_t, x_t, B_t, C_t = inp
                h = dA_t[:, :, None, None] * h + (dt_t[:, :, None] * x_t)[..., None] * B_t[:, None, None, :]
                y = jnp.einsum('bhdn,bn->bhd', h, C_t)
                return (h, y)
            xs = (dA.transpose(1, 0, 2), dt.transpose(1, 0, 2), xh.transpose(1, 0, 2, 3), Bm.transpose(1, 0, 2), Cm.transpose(1, 0, 2))
            h0 = jnp.zeros((b, NH, HD, DS), u.dtype)
            _, ys = lax.scan(step, h0, xs)
            y = ys.transpose(1, 0, 2, 3) + Dp[None, None, :, None] * xh
            y = y.reshape(b, L, DIN) * jax.nn.silu(z)
            y = y * lax.rsqrt(jnp.mean(y * y, -1, keepdims=True) + 1e-05) * nw
            return y @ Wo

        def _forward(x, pos_proj_w, local_w, W_in, conv_w, A_log, dt_bias, Dp, norm_w, W_out, se_w1, se_b1, se_w2, se_b2, proj_w, gn_gamma, gn_beta):
            xp = x + jnp.einsum('chw,oc->ohw', POS.astype(x.dtype), pos_proj_w)[None]
            local = jax.nn.gelu(lax.conv_general_dilated(xp, local_w, (1, 1), 'SAME', dimension_numbers=('NCHW', 'OIHW', 'NCHW'), feature_group_count=C))
            seq = xp.reshape(B, C, H * W).transpose(0, 2, 1)
            branches = [local]
            for i in range(4):
                u = jnp.take(seq, PERMS[i], axis=1)
                y = _mamba(u, W_in[i], conv_w[i], A_log[i], dt_bias[i], Dp[i], norm_w[i], W_out[i])
                y = jnp.take(y, INVS[i], axis=1)
                branches.append(y.transpose(0, 2, 1).reshape(B, C, H, W))
            stacked = jnp.stack(branches, 1)
            desc = stacked.mean(axis=(2, 3, 4))
            wts = jax.nn.sigmoid(jax.nn.gelu(desc @ se_w1 + se_b1) @ se_w2 + se_b2)
            fused = (stacked * wts[:, :, None, None, None]).sum(1)
            concat = stacked.reshape(B, NBR * C, H, W)
            proj = jnp.einsum('bihw,oi->bohw', concat, proj_w)
            g = proj.reshape(B, GN_GROUPS, -1)
            g = (g - g.mean(-1, keepdims=True)) * lax.rsqrt(g.var(-1, keepdims=True) + 1e-05)
            proj = jax.nn.gelu(g.reshape(B, C, H, W) * gn_gamma[None, :, None, None] + gn_beta[None, :, None, None])
            return x + fused + proj
        return _forward(x, pos_proj_w, local_w, W_in, conv_w, A_log, dt_bias, Dp, norm_w, W_out, se_w1, se_b1, se_w2, se_b2, proj_w, gn_gamma, gn_beta)

    def _gn(v, G=32, eps=1e-5):
        B_, C_, H_, W_ = v.shape
        g = v.reshape(B_, G, C_ // G, H_, W_)
        m = jnp.mean(g, axis=(2, 3, 4), keepdims=True)
        s = jnp.var(g, axis=(2, 3, 4), keepdims=True)
        return ((g - m) / jnp.sqrt(s + eps)).reshape(v.shape)

    def _ln_c(v, eps=1e-6):
        m = jnp.mean(v, axis=1, keepdims=True)
        s = jnp.var(v, axis=1, keepdims=True)
        return (v - m) / jnp.sqrt(s + eps)

    def _ln_t(v, eps=1e-5):
        m = jnp.mean(v, axis=-1, keepdims=True)
        s = jnp.var(v, axis=-1, keepdims=True)
        return (v - m) / jnp.sqrt(s + eps)

    def _to_tokens(v):
        B_, C_, H_, W_ = v.shape
        return v.reshape(B_, C_, H_ * W_).transpose(0, 2, 1)
    def _from_tokens(t, like):
        B_, C_, H_, W_ = like.shape
        return t.transpose(0, 2, 1).reshape(B_, C_, H_, W_)

    x = _L0_conv_ref(x, L0_conv_pos_proj_w, L0_conv_local_w, L0_conv_W_in, L0_conv_conv_w, L0_conv_A_log, L0_conv_dt_bias, L0_conv_Dp, L0_conv_norm_w, L0_conv_W_out, L0_conv_se_w1, L0_conv_se_b1, L0_conv_se_w2, L0_conv_se_b2, L0_conv_proj_w, L0_conv_gn_gamma, L0_conv_gn_beta)
    return x


_drawn_inputs = setup_inputs


def setup_inputs(seed=0):
    import zlib

    import numpy as np

    out = dict(_drawn_inputs(seed))
    spreads = {'L0_conv_gn_gamma': (1.0, 0.2), 'L0_conv_gn_beta': (0.0, 0.1)}
    factors = {'L0_conv_norm_w': 4.268,
     'L0_conv_se_w1': 8.0,
     'L0_conv_se_b1': 8.0,
     'L0_conv_se_w2': 8.0,
     'L0_conv_se_b2': 3.279}
    for name, (base, spread) in spreads.items():
        noise = np.random.default_rng([zlib.crc32(name.encode()), seed]).standard_normal(out[name].shape)
        drawn = base * np.exp(spread * noise) if base else spread * noise
        out[name] = jnp.asarray(drawn.astype(out[name].dtype))
    for name, factor in factors.items():
        out[name] = (out[name] * factor).astype(out[name].dtype)
    return out
```

```python
from contextlib import ExitStack

import numpy as np
import concourse.bass as bass
from concourse import mybir

F32 = mybir.dt.float32
BF16 = mybir.dt.bfloat16
ALU = mybir.AluOpType
ACT = mybir.ActivationFunctionType
AX_X = mybir.AxisListType.X

BATCH, CH, HEIGHT, WIDTH = 8, 128, 64, 64
PIX = HEIGHT * WIDTH
DIRS = 4
STATE = 64
HEADS, HEAD = 8, 32
INNER = HEADS * HEAD
CONV = INNER + 2 * STATE
XBLK = CONV // 128
TAPS = 4
CHUNK = 128
TILE = 512
CPT = TILE // CHUNK
TPD = PIX // TILE
TILES = DIRS * TPD
NCHUNK = PIX // CHUNK
BRANCHES = 5
GROUP = CH // 8
REP = 4
SPLIT = 3
EPS = 1e-5

C_IDENT, C_TRI, C_LAST, C_GROUP, C_POS = 0, 128, 256, 384, 512
C_SEL, C_NEG, C_FLAG, C_GE1, C_GE2, C_GE0 = 576, 608, 640, 680, 681, 682
C_COLS = 683
V_ALOG, V_DTB, V_DP, V_W1, V_B1, V_W2, V_B2 = 0, 32, 64, 96, 106, 108, 118
V_COLS = 123


def shape_constants():
    t = np.zeros((128, C_COLS), np.float32)
    i = np.arange(128)
    t[:, C_IDENT:C_IDENT + 128] = np.eye(128)
    t[:, C_TRI:C_TRI + 128] = -1e30 * (i[None, :] < i[:, None])
    t[127, C_LAST:C_LAST + 128] = 1.0
    t[:, C_GROUP:C_GROUP + 128] = (i[:, None] // GROUP == i[None, :] // GROUP) / GROUP
    half = CH // 2
    freq = 10000.0 ** (np.arange(0, half, 2, dtype=np.float32) / half)
    ph = np.arange(HEIGHT, dtype=np.float32)[:, None] / freq
    emb = np.stack([np.sin(ph), np.cos(ph)], 2).reshape(HEIGHT, -1).T
    t[0:64, C_POS:C_POS + 64] = emb
    t[64:128, C_POS:C_POS + 64] = emb
    row_dir, row_rep, row_head = i // 32, i // 8 % 4, i % 8
    for d in range(DIRS):
        for h in range(HEADS):
            own = (row_dir == d) & (row_head == h) & (row_rep < SPLIT)
            t[:, C_SEL + 8 * d + h] = own
            t[:, C_NEG + 8 * d + h] = -1.0 * own
    t[:, C_FLAG:C_FLAG + 40] = np.arange(40) % TPD != 0
    t[:, C_GE0] = -1.0 * (row_rep < SPLIT)
    t[:, C_GE1] = -1.0 * (row_rep >= 1)
    t[:, C_GE2] = -1.0 * (row_rep >= 2)
    return t


def build(nc, a, out):
    ctx = ExitStack()
    with ctx:
        def sb(name, shape, dt=F32):
            return ctx.enter_context(nc.sbuf_tensor(name, shape, dt))

        def sem(name):
            return ctx.enter_context(nc.semaphore(name))

        useq = sb("useq", [128, DIRS * PIX])
        local = sb("local", [128, PIX])
        arena1 = sb("arena1", [128, PIX])
        arena2 = sb("arena2", [128, 3 * (3 + TILE) + 6 * TILE])
        csp = sb("csp", [128, PIX], BF16)
        sel = sb("sel", [128, DIRS * HEADS * 128], BF16)
        ident_b = sb("ident_b", [128, 128], BF16)
        later = sb("later", [128, 128], BF16)
        neg = sb("neg", [128, DIRS * HEADS], BF16)
        const = sb("const", [128, C_COLS])
        vbc = sb("vbc", [128, V_COLS])
        ones = sb("ones", [128, 128])
        dt_tok = sb("dt_tok", [128, DIRS * NCHUNK * HEADS])
        ecs_tok = sb("ecs_tok", [128, DIRS * NCHUNK * HEADS])
        wdt_tok = sb("wdt_tok", [128, DIRS * NCHUNK * HEADS])
        dec_bc = sb("dec_bc", [128, DIRS * NCHUNK * HEADS])
        wz = sb("wz", [128, DIRS * INNER])
        wo_all = sb("wo_all", [128, DIRS * 2 * CH])
        wdt = sb("wdt", [128, DIRS * 32])
        wx = sb("wx", [128, CONV])
        wo = sb("wo", [128, 2 * CH])
        taps = sb("taps", [128, DIRS * XBLK * TAPS])
        lw = sb("lw", [128, 9])
        pw_t = sb("pw_t", [128, BRANCHES * CH])
        posw_t = sb("posw_t", [128, CH])
        pos = sb("pos", [128, 2 * 64])
        gnp = sb("gnp", [128, 2])
        nw_t = sb("nw_t", [128, 8])
        dirpar = sb("dirpar", [128, 2])
        sums = sb("sums", [128, BRANCHES * TPD])
        small = sb("small", [128, 64])
        ucur = sb("ucur", [128, TILE])
        xs = sb("xs", [128, CPT * CONV])
        cs_ = sb("c_low", [64, CPT * CHUNK])
        c_use = sb("c_use", [64, 2 * CHUNK])
        xbg = sb("xbg", [128, 2 * 448])
        xdt = sb("xdt", [128, 2 * INNER])
        xw = sb("xw", [128, 2 * INNER])
        xd = sb("xd", [128, 2 * INNER])
        thz = sb("thz", [128, 2 * INNER])
        y1 = sb("y1", [128, INNER])
        y2 = sb("y2", [128, 2 * INNER])
        gate = sb("gate", [128, CPT * INNER])
        yg = sb("yg", [128, 2 * INNER])
        yr = sb("yr", [128, 2 * INNER])
        ynt = sb("ynt", [128, 2 * TILE])
        st = sb("st", [64, 2 * INNER])
        st_dec = sb("st_dec", [64, INNER])
        sq_out = sb("sq_out", [128, INNER])
        ps = ctx.enter_context(nc.psum_tensor("ps", [128, 8 * 512], F32))

        def bank(n, lo=0, hi=512):
            return ps[:, 512 * n + lo:512 * n + hi]

        B_P, B_T, B_D, B_Y, B_S, B_C, B_O = 0, 1, 2, 4, 5, 6, 7

        ident = const[:, C_IDENT:C_IDENT + 128]
        decay = arena1[:, 0:2048].rearrange("p (b h t) -> p b h t", b=2, h=HEADS)
        mix = arena1[:, 2048:4096].rearrange("p (b h t) -> p b h t", b=2, h=HEADS)
        RAW = 3 + TILE
        raw = arena2[:, 0:3 * RAW].rearrange("p (j t) -> p j t", j=XBLK)
        conv = arena2[:, 3 * RAW:3 * RAW + 3 * TILE].rearrange("p (j t) -> p j t", j=XBLK)
        tanh = arena2[:, 3 * RAW + 3 * TILE:3 * RAW + 6 * TILE].rearrange("p (j t) -> p j t", j=XBLK)
        xs_v = xs[:, :].rearrange("p (c j t) -> p c j t", c=CPT, j=XBLK)
        seq = useq[:, :].rearrange("p (d n) -> p d n", d=DIRS)
        work1, work2 = arena1[:, :], arena2[:, 0:PIX]
        vrow = arena2[0:1, 128:128 + V_COLS]

        S = {n: sem(n) for n in (
            "phase", "loaded", "setup_step", "x_loaded", "prep_step", "local_step", "scan_step",
            "post_step", "proj_ready", "proj_evac", "fuse_step", "stored", "part_ready",
            "wx_loaded", "wo_loaded", "ucur_loaded", "xbc_ready", "z_ready", "xbc_evac", "z_evac",
            "thz_ready", "tap_done", "conv_done", "tanh_done", "silu_done", "tbank_ready", "d_ready",
            "xbg_ready", "l_ready", "x_ready", "m_ready", "st_ready", "sdec_ready",
            "s_upd", "b_done", "y1_done", "ysum_done", "y3_done", "yg_ready", "ss_ready",
            "var_done", "r_ready", "yr_ready", "yt_ready", "yt_evac", "out_ready", "o_evac",
            "stat_step", "settled")}

        SETUP_BARS, BATCH_BARS = 7, 17

        def settle(eng):
            eng.sem_inc(S["settled"], 1)

        def barrier(eng, count):
            eng.drain().then_inc(S["phase"], 1)
            eng.wait_ge(S["phase"], 5 * (count + 1))
            settle(eng)

        def bar(eng, b, n):
            barrier(eng, SETUP_BARS + b * BATCH_BARS + n)

        def alive(t):
            return not isinstance(t, int) or 0 <= t < TILES

        def first(t):
            return isinstance(t, int) and t == 0

        def lagged(t, c, lag):
            return (t, c - lag) if c >= lag else (t - 1, c - lag + CPT)

        def tile_no(b, t):
            return b * TILES + t

        def chunk_no(b, t, c):
            return (b * TILES + t) * CPT + c

        def earlier(eng, name, b, t, c, lag):
            if not (first(t) and c < lag):
                eng.wait_ge(S[name], chunk_no(b, t, c) - lag + 1)

        def heads(ap, n=HEAD):
            p, h = ap.shape
            return ap.unsqueeze(2).broadcast_to([p, h, n])

        def by_head(ap):
            return ap.rearrange("p (h d) -> p h d", h=HEADS)

        def table(tab, t, c, rows=128):
            return heads(tab[0:rows, bass.ds((t * CPT + c) * HEADS, HEADS)])

        def buf(t_, c, w):
            return t_[:, (c % 2) * w:(c % 2) * w + w]

        def run_tiles(eng, b, body):
            for t in (-1, 0, 1):
                body(eng, b, t)
            with eng.Fori(2, 30) as t:
                body(eng, b, t)
            for t in (30, 31, 32, 33):
                body(eng, b, t)

        def sp_setup(sp):
            L = S["loaded"]
            sp.dma_start(const[:, :], a["shape_const"]).then_inc(L, 16)
            for name, at, n in (("A_log", V_ALOG, 32), ("dt_bias", V_DTB, 32), ("Dp", V_DP, 32)):
                sp.dma_start(vrow[0:1, at:at + n], a[name].rearrange("(o d) h -> o (d h)", o=1)).then_inc(L, 16)
            for name, at, n in (("se_w1", V_W1, 10), ("se_w2", V_W2, 10)):
                sp.dma_start(vrow[0:1, at:at + n], a[name].rearrange("(o d) h -> o (d h)", o=1)).then_inc(L, 16)
            for name, at, n in (("se_b1", V_B1, 2), ("se_b2", V_B2, 5)):
                sp.dma_start(vrow[0:1, at:at + n], a[name].rearrange("(o d) -> o d", o=1)).then_inc(L, 16)
            w_in = a["W_in"].rearrange("d c n -> c d n")
            sp.dma_start(wz[:, :].rearrange("p (d n) -> p d n", d=DIRS), w_in[:, :, 0:INNER]).then_inc(L, 16)
            sp.dma_start(small[:, 0:32].rearrange("p (d n) -> p d n", d=DIRS),
                         w_in[:, :, INNER + CONV:INNER + CONV + HEADS]).then_inc(L, 16)
            sp.dma_start(wo_all[:, :].rearrange("p (d m o) -> p d m o", d=DIRS, m=2),
                         a["W_out"].rearrange("d (m k) o -> k d m o", m=2)).then_inc(L, 16)
            sp.dma_start(lw[:, :], a["local_w"].rearrange("c u i j -> c (u i j)")).then_inc(L, 16)
            sp.dma_start(gnp[:, 0:1], a["gn_gamma"].rearrange("(c o) -> c o", o=1)).then_inc(L, 16)
            sp.dma_start(gnp[:, 1:2], a["gn_beta"].rearrange("(c o) -> c o", o=1)).then_inc(L, 16)
            sp.dma_start(arena1[:, 0:640], a["proj_w"]).then_inc(L, 16)
            sp.dma_start(arena1[:, 640:768], a["pos_proj_w"]).then_inc(L, 16)
            sp.dma_start(arena1[0:8, 768:896], a["norm_w"].rearrange("d (m k) -> (d m) k", m=2)).then_inc(L, 16)
            sp.dma_start(arena1[0:16, 1024:1024 + CONV], a["conv_w"].rearrange("d k c -> (d k) c")).then_inc(L, 16)
            sp.wait_ge(L, 16 * 18)
            for n in range(SETUP_BARS):
                barrier(sp, n)

        def sp_body(sp, b, t):
            i = t + 1
            if alive(t - 1):
                if not first(t - 1):
                    sp.wait_ge(S["out_ready"], tile_no(b, t - 1))
                sp.dma_start(wo[:, :], wo_all[:, bass.ds((t - 1) // TPD * 2 * CH, 2 * CH)]).then_inc(S["wo_loaded"], 16)
            if alive(i):
                if not first(i):
                    sp.wait_ge(S["z_ready"], 2 * tile_no(b, i))
                sp.dma_start(ucur[:, :], useq[:, bass.ds(i * TILE, TILE)]).then_inc(S["ucur_loaded"], 16)
            if alive(i + 1):
                sp.wait_ge(S["xbc_ready"], 3 * tile_no(b, i) + 3)
                load_wx(sp, i + 1)

        def load_wx(sp, i):
            d = i // TPD
            w = a["W_in"][d, :, INNER:INNER + CONV] if isinstance(d, int) else \
                a["W_in"][bass.ds(d, 1), :, INNER:INNER + CONV].rearrange("d c n -> c (d n)")
            sp.dma_start(wx[:, :], w).then_inc(S["wx_loaded"], 16)

        def sp_program(sp):
            sp_setup(sp)
            with sp.Fori(0, BATCH) as b:
                x_img = a["x"][bass.ds(b, 1)].rearrange("b c h w -> c (b h w)")
                sp.dma_start(seq[:, 0, :], x_img).then_inc(S["x_loaded"], 16)
                sp.wait_ge(S["x_loaded"], 32 * b + 16)
                settle(sp)
                for n in range(15):
                    bar(sp, b, n)
                load_wx(sp, 0)
                run_tiles(sp, b, sp_body)
                bar(sp, b, 15)
                sp.dma_start(work2, x_img).then_inc(S["x_loaded"], 16)
                sp.wait_ge(S["x_loaded"], 32 * b + 32)
                out_img = out[bass.ds(b, 1)].rearrange("b c h w -> c (b h w)")
                for q in range(4):
                    sp.wait_ge(S["part_ready"], 4 * b + q + 1)
                    sp.dma_start(out_img[:, q * 1024:(q + 1) * 1024], work2[:, q * 1024:(q + 1) * 1024])\
                        .then_inc(S["stored"], 16)
                sp.wait_ge(S["stored"], 64 * b + 64)
                settle(sp)
                bar(sp, b, 16)

        def pe_setup(pe):
            barrier(pe, 0)
            mm = nc.tensor
            for k in range(BRANCHES):
                mm.transpose(bank(k, 0, 128), arena1[:, 128 * k:128 * k + 128], ident)
            mm.transpose(bank(5, 0, 128), arena1[:, 640:768], ident)
            mm.transpose(bank(6, 0, 8), arena1[0:8, 768:896], ident[0:8, 0:8])
            for j in range(XBLK):
                mm.transpose(bank(6, 16 + 16 * j, 32 + 16 * j), arena1[0:16, 1024 + 128 * j:1152 + 128 * j],
                             ident[0:16, 0:16])
            mm.matmul(bank(7, 0, V_COLS), ones[0:1, :], vrow[0:1, :], start=True, stop=True)
            barrier(pe, 1)
            barrier(pe, 2)
            mm.matmul(bank(0, 0, 64), posw_t[0:64, :], const[0:64, C_POS:C_POS + 64], start=True, stop=True)
            mm.matmul(bank(1, 0, 64), posw_t[64:128, :], const[64:128, C_POS:C_POS + 64], start=True, stop=True)
            for n in range(3, SETUP_BARS):
                barrier(pe, n)

        def pe_prep(pe, b):
            mm = nc.tensor
            bar(pe, b, 0)
            bar(pe, b, 1)
            bar(pe, b, 2)
            for q in range(TPD):
                for d in range(DIRS):
                    mm.matmul(ps[32 * d:32 * d + 32, 512 * q:512 * q + 512], wdt[:, 32 * d:32 * d + 32],
                              seq[:, d, 512 * q:512 * q + 512], start=True, stop=True)
            bar(pe, b, 3)
            bar(pe, b, 4)
            bar(pe, b, 5)
            for j in range(NCHUNK):
                mm.transpose(ps[:, 128 * j:128 * j + 128], work2[:, 128 * j:128 * j + 128], ident)
            bar(pe, b, 6)
            bar(pe, b, 7)
            for j in range(NCHUNK):
                mm.transpose(ps[:, 128 * j:128 * j + 128], work1[:, 128 * j:128 * j + 128], ident)
            bar(pe, b, 8)
            bar(pe, b, 9)
            for q in range(2):
                mm.matmul(bank(q), const[:, C_LAST:C_LAST + 128], wdt_tok[:, 512 * q:512 * q + 512],
                          start=True, stop=True)
            for n in range(10, 15):
                bar(pe, b, n)

        def pe_body(pe, b, t):
            mm = nc.tensor
            i = t + 1
            xs_t = xs_v
            for c in range(CPT):
                if c == 0 and alive(t - 2):
                    n = tile_no(b, t - 2)
                    pe.wait_ge(S["yt_evac"], CPT * n + CPT)
                    pe.wait_ge(S["wo_loaded"], 16 * n + 16)
                    if not first(t - 2):
                        pe.wait_ge(S["o_evac"], n)
                    mm.matmul(bank(B_O), wo[:, 0:128], ynt[:, 0:TILE], start=True, stop=False)
                    mm.matmul(bank(B_O), wo[:, 128:256], ynt[:, TILE:2 * TILE], start=False, stop=True)\
                        .then_inc(S["out_ready"], 1)
                if c == 1 and alive(i - 1):
                    n = tile_no(b, i - 1)
                    if alive(i):
                        pe.wait_ge(S["xbc_evac"], 3 * tile_no(b, i) + 1)
                    else:
                        pe.wait_ge(S["z_evac"], 2 * n + 1)
                    project_z(pe, b, i - 1, 1)
                if c < XBLK and alive(i):
                    n = tile_no(b, i)
                    if c == 0:
                        pe.wait_ge(S["wx_loaded"], 16 * n + 16)
                        if not first(i):
                            pe.wait_ge(S["z_evac"], 2 * n - 1)
                    elif c == 1:
                        if first(i):
                            pe.wait_ge(S["xbc_evac"], 3 * n + 1)
                        else:
                            pe.wait_ge(S["z_evac"], 2 * n)
                    else:
                        pe.wait_ge(S["xbc_evac"], 3 * n + 2)
                    mm.matmul(bank(B_P), wx[:, 128 * c:128 * c + 128], useq[:, bass.ds(i * TILE, TILE)],
                              start=True, stop=True).then_inc(S["xbc_ready"], 1)
                if c == 3 and alive(i):
                    pe.wait_ge(S["xbc_evac"], 3 * tile_no(b, i) + 3)
                    pe.wait_ge(S["ucur_loaded"], 16 * tile_no(b, i) + 16)
                    project_z(pe, b, i, 0)
                if alive(t):
                    k = chunk_no(b, t, c)
                    pe.wait_ge(S["silu_done"], k + 1)
                    earlier(pe, "xbg_ready", b, t, c, 1)
                    for j in range(2):
                        mm.transpose(bank(B_T, 128 * j, 128 * j + 128), xs_t[:, c, j, :], ident)
                    mm.transpose(bank(B_T, 256, 320), xs_t[0:64, c, 2, :], ident[0:64, 0:64])
                    mm.matmul(bank(B_T, 320, 448), xs_t[0:64, c, 2, :], cs_[:, 128 * c:128 * c + 128],
                              start=True, stop=True).then_inc(S["tbank_ready"], 1)
                    earlier(pe, "l_ready", b, t, c, 1)
                    d = t // TPD
                    cols = csp[:, bass.ds(t % TPD * TILE + c * CHUNK, CHUNK)]
                    for q in range(2):
                        for h in range(4):
                            mm.matmul(bank(B_D + q, 128 * h, 128 * h + 128),
                                      sel[:, bass.ds((d * HEADS + 4 * q + h) * 128, 128)], cols,
                                      start=(h == 0), stop=False, skip_group_check=True)
                        mm.matmul(bank(B_D + q), ident_b[:, :], later[:, :].unsqueeze(1).broadcast_to([128, 4, 128]),
                                  start=False, stop=False, skip_group_check=True)
                        last = mm.matmul(bank(B_D + q), cols,
                                         neg[:, bass.ds(d * HEADS + 4 * q, 4)].unsqueeze(2)
                                         .broadcast_to([128, 4, 128]),
                                         start=False, stop=True, skip_group_check=True)
                    last.then_inc(S["d_ready"], 1)
                tb, cb = lagged(t, c, 1)
                if alive(tb):
                    k = chunk_no(b, tb, cb)
                    pe.wait_ge(S["x_ready"], k + 1)
                    earlier(pe, "s_upd", b, tb, cb, 1)
                    mm.matmul(ps[0:64, 512 * B_S:512 * B_S + INNER],
                              buf(xbg, cb, 448)[:, 256:320], buf(xw, cb, INNER), start=True, stop=True)\
                        .then_inc(S["st_ready"], 1)
                    pe.wait_ge(S["m_ready"], k + 1)
                    earlier(pe, "ysum_done", b, tb, cb, 1)
                    for h in range(HEADS):
                        mm.matmul(bank(B_Y, HEAD * h, HEAD * h + HEAD), mix[:, cb % 2, h, :],
                                  buf(xdt, cb, INNER)[:, HEAD * h:HEAD * h + HEAD], start=True, stop=True)
                    mm.matmul(bank(B_Y, 256, 512), buf(c_use, cb, CHUNK), buf(st, cb, INNER),
                              start=True, stop=True).then_inc(S["b_done"], 1)
                tc_, cc = lagged(t, c, 3)
                if alive(tc_):
                    k = chunk_no(b, tc_, cc)
                    pe.wait_ge(S["yr_ready"], k + 1)
                    earlier(pe, "yt_evac", b, tc_, cc, 1)
                    mm.transpose(bank(B_C, 0, 128), buf(yr, cc, INNER)[:, 0:128], ident)
                    mm.transpose(bank(B_C, 128, 256), buf(yr, cc, INNER)[:, 128:256], ident)\
                        .then_inc(S["yt_ready"], 1)

        def project_z(pe, b, i, pair):
            w = wz[:, bass.ds(i // TPD * INNER, INNER)]
            for q in range(2):
                col = (2 * pair + q) * CHUNK
                last = nc.tensor.matmul(bank(B_P, q * INNER, q * INNER + INNER), ucur[:, col:col + CHUNK], w,
                                        start=True, stop=True)
            last.then_inc(S["z_ready"], 1)

        def even_odd(view):
            return ((view[:, 0::2, :], False), (view[:, 1::2, :], True))

        def image_rows(d, q):
            v = seq[:, d, :].rearrange("p (a b) -> p a b", b=64)
            if d == 0:
                return [(v[:, 8 * q:8 * q + 8, :], slice(0, 8), slice(0, 64))]
            if d == 1:
                return [(v[:, :, 8 * q:8 * q + 8].rearrange("p w h -> p h w"), slice(0, 8), slice(0, 64))]
            if d == 2:
                return [(v[:, 8 * q:8 * q + 8:2, :], slice(0, 8, 2), slice(0, 64)),
                        (v[:, 8 * q + 1:8 * q + 8:2, ::-1], slice(1, 8, 2), slice(0, 64))]
            hi, lo = 63 - 8 * q, 63 - 8 * q - 8
            back = v[:, 1::2, hi:lo:-1] if lo >= 0 else v[:, 1::2, hi::-1]
            return [(v[:, 0::2, 8 * q:8 * q + 8].rearrange("p w h -> p h w"), slice(0, 8), slice(0, 64, 2)),
                    (back.rearrange("p w h -> p h w"), slice(0, 8), slice(1, 64, 2))]

        POST = 14

        def step(eng, b, n):
            eng.wait_ge(S["post_step"], POST * b + n)

        def pe_post(pe, b):
            mm = nc.tensor
            bar(pe, b, 15)
            for q in range(TPD):
                o = bank(q % 4).rearrange("p (h w) -> p h w", w=64)
                n = TPD * b + q
                if q >= 4:
                    pe.wait_ge(S["proj_evac"], n - 3)
                for d in range(DIRS):
                    for src, rows, cols in image_rows(d, q):
                        mm.matmul(o[:, rows, cols], pw_t[:, 128 * (d + 1):128 * (d + 2)], src,
                                  start=(d == 0), stop=False, skip_group_check=True)
                mm.matmul(bank(q % 4), pw_t[:, 0:128], local[:, 512 * q:512 * q + 512], start=False, stop=True,
                          skip_group_check=True).then_inc(S["proj_ready"], 1)
            step(pe, b, 1)
            mm.matmul(bank(4, 0, BRANCHES), ones[:, :], small[:, 0:5], start=True, stop=True)\
                .then_inc(S["post_step"], 1)
            step(pe, b, 9)
            mm.matmul(bank(5, 0, 1), const[:, C_GROUP:C_GROUP + 128], small[:, 20:21], start=True, stop=True)\
                .then_inc(S["post_step"], 1)
            step(pe, b, 12)
            mm.matmul(bank(6, 0, 1), const[:, C_GROUP:C_GROUP + 128], small[:, 24:25], start=True, stop=True)\
                .then_inc(S["post_step"], 1)
            bar(pe, b, 16)

        def pe_program(pe):
            pe_setup(pe)
            with pe.Fori(0, BATCH) as b:
                pe_prep(pe, b)
                run_tiles(pe, b, pe_body)
                pe_post(pe, b)

        def act_setup(act):
            barrier(act, 0)
            barrier(act, 1)
            barrier(act, 2)
            barrier(act, 3)
            barrier(act, 4)
            act.activation(small[:, 43:44], small[:, 41:42], ACT.Exp)
            barrier(act, 5)
            barrier(act, 6)

        def act_prep(act, b):
            bar(act, b, 0)
            bar(act, b, 1)
            img = seq[:, 0, :].rearrange("p (h w) -> p h w", w=64)
            act.activation(seq[:, 1, :].rearrange("p (w h) -> p h w", h=64), img, ACT.Copy)
            bar(act, b, 2)
            act.activation(local[:, :], local[:, :], ACT.Gelu_apprx_tanh, accum_out=sums[:, 0:1])
            bar(act, b, 3)
            P_ = S["prep_step"]
            act.activation(work1, ps[:, :], ACT.Abs, bias=dirpar[:, 1:2]).then_inc(P_, 1)
            act.activation(work2, ps[:, :], ACT.Relu, bias=dirpar[:, 1:2])
            act.wait_ge(P_, 3 * b + 1)
            act.activation(work1, work1, ACT.Exp, scale=-1.0).then_inc(P_, 1)
            act.wait_ge(P_, 3 * b + 2)
            act.activation(work1, work1, ACT.Ln, bias=1.0).then_inc(P_, 1)
            bar(act, b, 4)
            bar(act, b, 5)
            bar(act, b, 6)
            tok = ps[:, :].rearrange("p (j d r h) -> p j d r h", j=NCHUNK, d=DIRS, r=REP)
            for d in range(DIRS):
                act.activation(tab_view(wdt_tok)[:, d], tok[:, :, d, 0, :], ACT.Copy)
                act.activation(tab_view(ecs_tok)[:, d], tok[:, :, d, 0, :], ACT.Exp)
            bar(act, b, 7)
            bar(act, b, 8)
            bar(act, b, 9)
            bar(act, b, 10)
            act.activation(dec_bc[:, :], ps[:, 0:1024], ACT.Exp)
            bar(act, b, 11)
            bar(act, b, 12)
            act.activation(wdt_tok[:, :], wdt_tok[:, :], ACT.Exp)
            bar(act, b, 13)
            bar(act, b, 14)

        def tab_view(tab):
            return tab[:, :].rearrange("p (d j h) -> p d j h", d=DIRS, j=NCHUNK)

        def act_body(act, b, t):
            i = t + 1
            for c in range(CPT):
                if c == 1 and alive(i - 1):
                    evac_z(act, b, i - 1, 1)
                if c < XBLK and alive(i):
                    n = tile_no(b, i)
                    act.wait_ge(S["xbc_ready"], 3 * n + c + 1)
                    if not first(i):
                        act.wait_ge(S["conv_done"], 3 * n + c - 2)
                    act.activation(raw[:, c, 3:3 + TILE], bank(B_P), ACT.Copy).then_inc(S["xbc_evac"], 1)
                ty, cy = lagged(t, c, 3)
                if alive(ty):
                    k = chunk_no(b, ty, cy)
                    act.wait_ge(S["r_ready"], k + 1)
                    earlier(act, "yt_ready", b, ty, cy, 2)
                    act.activation(buf(yr, cy, INNER), buf(yg, cy, INNER), ACT.Copy,
                                   scale=small[:, 36 + cy % 2:37 + cy % 2]).then_inc(S["yr_ready"], 1)
                if alive(t):
                    k = chunk_no(b, t, c)
                    act.wait_ge(S["tbank_ready"], k + 1)
                    earlier(act, "x_ready", b, t, c, 2)
                    earlier(act, "st_ready", b, t, c, 2)
                    earlier(act, "m_ready", b, t, c, 2)
                    act.activation(buf(xbg, c, 448), bank(B_T, 0, 448), ACT.Copy).then_inc(S["xbg_ready"], 1)
                    act.wait_ge(S["d_ready"], k + 1)
                    earlier(act, "m_ready", b, t, c, 2)
                    act.activation(decay[:, c % 2].rearrange("p h t -> p (h t)"), ps[:, 512 * B_D:512 * B_D + 1024],
                                   ACT.Exp).then_inc(S["l_ready"], 1)
                if 1 <= c <= XBLK and alive(i):
                    n = tile_no(b, i)
                    act.wait_ge(S["conv_done"], 3 * n + c)
                    if not first(i):
                        act.wait_ge(S["silu_done"], CPT * n)
                    act.activation(tanh[:, c - 1, :], conv[:, c - 1, :], ACT.Tanh).then_inc(S["tanh_done"], 1)
                tq, cq = lagged(t, c, 2)
                if alive(tq):
                    k = chunk_no(b, tq, cq)
                    act.wait_ge(S["yg_ready"], k + 1)
                    earlier(act, "r_ready", b, tq, cq, 2)
                    act.activation(sq_out[:, :], buf(yg, cq, INNER), ACT.Square,
                                   accum_out=small[:, 32 + cq % 2:33 + cq % 2]).then_inc(S["ss_ready"], 1)
                te, ce = lagged(t, c, 4)
                if alive(te):
                    k = chunk_no(b, te, ce)
                    act.wait_ge(S["yt_ready"], k + 1)
                    if ce == 0 and not first(te):
                        act.wait_ge(S["out_ready"], tile_no(b, te))
                    act.activation(ynt[:, :].rearrange("p (m t) -> p m t", m=2)[:, :, 128 * ce:128 * ce + 128],
                                   bank(B_C, 0, 256).rearrange("p (m t) -> p m t", m=2), ACT.Copy)\
                        .then_inc(S["yt_evac"], 1)
                if c == 0 and alive(t - 2):
                    n = tile_no(b, t - 2)
                    act.wait_ge(S["out_ready"], n + 1)
                    act.activation(useq[:, bass.ds((t - 2) * TILE, TILE)], bank(B_O), ACT.Copy,
                                   accum_out=sums[:, bass.ds(TPD + (t - 2), 1)]).then_inc(S["o_evac"], 1)
                if c == 3 and alive(i):
                    evac_z(act, b, i, 0)

        def evac_z(act, b, i, pair):
            n = tile_no(b, i)
            act.wait_ge(S["z_ready"], 2 * n + pair + 1)
            act.activation(thz[:, :], bank(B_P), ACT.Tanh, scale=0.5).then_inc(S["thz_ready"], 1)

        def act_post(act, b):
            bar(act, b, 15)
            for q in range(TPD):
                act.wait_ge(S["proj_ready"], TPD * b + q + 1)
                act.activation(work1[:, 512 * q:512 * q + 512], bank(q % 4), ACT.Copy).then_inc(S["proj_evac"], 1)
            step(act, b, 4)
            act.activation(small[:, 8:10], small[:, 8:10], ACT.Gelu_apprx_tanh).then_inc(S["post_step"], 1)
            step(act, b, 6)
            act.activation(small[:, 12:17], small[:, 12:17], ACT.Tanh, scale=0.5).then_inc(S["post_step"], 1)
            step(act, b, 14)
            for q in range(4):
                act.activation(work1[:, 1024 * q:1024 * q + 1024], work1[:, 1024 * q:1024 * q + 1024],
                               ACT.Gelu_apprx_tanh, scale=small[:, 28:29], bias=small[:, 29:30])\
                    .then_inc(S["stat_step"], 1)
            bar(act, b, 16)

        def act_program(act):
            act_setup(act)
            with act.Fori(0, BATCH) as b:
                act_prep(act, b)
                run_tiles(act, b, act_body)
                act_post(act, b)

        def dve_setup(dve):
            v = nc.vector
            v.memset(ones[:, :], 1.0)
            v.memset(small[:, 32:64], -0.5)
            v.memset(st[:, :], 0.0)
            barrier(dve, 0)
            barrier(dve, 1)
            v.tensor_copy(pw_t[:, :].rearrange("p (k o) -> p k o", k=BRANCHES),
                          ps[:, 0:BRANCHES * 512].rearrange("p (k o) -> p k o", k=BRANCHES)[:, :, 0:128])
            v.tensor_copy(posw_t[:, :], bank(5, 0, 128))
            v.tensor_copy(nw_t[:, :], bank(6, 0, 8))
            v.tensor_scalar(taps[:, :].rearrange("p (d j k) -> p d j k", d=DIRS, j=XBLK),
                            bank(6, 16, 64).rearrange("p (j d k) -> p d j k", j=XBLK, d=DIRS), 0.5, None, ALU.mult)
            v.tensor_copy(vbc[:, :], bank(7, 0, V_COLS))
            v.tensor_copy(wdt[:, :].rearrange("p (d r h) -> p d r h", d=DIRS, r=REP),
                          small[:, 0:32].rearrange("p (d h) -> p d h", d=DIRS).unsqueeze(2)
                          .broadcast_to([128, DIRS, REP, HEADS]))
            v.tensor_copy(ident_b[:, :], ident)
            v.tensor_copy(later[:, :], const[:, C_TRI:C_TRI + 128])
            v.tensor_copy(neg[:, :], const[:, C_NEG:C_NEG + 32])
            v.tensor_copy(sel[:, :].rearrange("p (n s) -> p n s", s=128),
                          const[:, C_SEL:C_SEL + 32].unsqueeze(2).broadcast_to([128, 32, 128]))
            barrier(dve, 2)
            v.tensor_tensor(arena2[:, 0:32], vbc[:, V_ALOG:V_ALOG + 32], const[:, C_SEL:C_SEL + 32], ALU.mult)
            v.tensor_tensor(arena2[:, 32:64], vbc[:, V_DTB:V_DTB + 32], const[:, C_SEL:C_SEL + 32], ALU.mult)
            for d in range(DIRS):
                for m in range(2):
                    w = wo_all[:, (2 * d + m) * CH:(2 * d + m + 1) * CH]
                    v.tensor_scalar(w, w, nw_t[:, 2 * d + m:2 * d + m + 1], None, ALU.mult)
            barrier(dve, 3)
            v.reduce_sum(small[:, 41:42], arena2[:, 0:32], AX_X)
            v.reduce_sum(dirpar[:, 1:2], arena2[:, 32:64], AX_X)
            v.tensor_copy(pos[:, 0:64], bank(0, 0, 64))
            v.tensor_copy(pos[:, 64:128], bank(1, 0, 64))
            barrier(dve, 4)
            barrier(dve, 5)
            v.tensor_tensor(dirpar[:, 0:1], small[:, 43:44], const[:, C_GE0:C_GE0 + 1], ALU.mult)
            barrier(dve, 6)

        def dve_prep(dve, b):
            v = nc.vector
            bar(dve, b, 0)
            img = seq[:, 0, :].rearrange("p (h w) -> p h w", w=64)
            LS = S["local_step"]
            n_local = 11
            v.tensor_tensor(img, img, pos[:, 0:64].unsqueeze(2).broadcast_to([128, 64, 64]), ALU.add).then_inc(LS, 1)
            dve.wait_ge(LS, n_local * b + 1)
            v.tensor_tensor(img, img, pos[:, 64:128].unsqueeze(1).broadcast_to([128, 64, 64]), ALU.add)\
                .then_inc(LS, 1)
            bar(dve, b, 1)
            acc = local[:, :].rearrange("p (h w) -> p h w", w=64)
            v.tensor_scalar(acc, img, lw[:, 4:5], None, ALU.mult).then_inc(LS, 1)
            n = 3
            for dh in (-1, 0, 1):
                for dw in (-1, 0, 1):
                    if dh == 0 and dw == 0:
                        continue
                    h0, h1 = max(0, -dh), 64 - max(0, dh)
                    w0, w1 = max(0, -dw), 64 - max(0, dw)
                    tap = 3 * (dh + 1) + dw + 1
                    dve.wait_ge(LS, n_local * b + n)
                    v.scalar_tensor_tensor(acc[:, h0:h1, w0:w1], img[:, h0 + dh:h1 + dh, w0 + dw:w1 + dw],
                                           lw[:, tap:tap + 1], acc[:, h0:h1, w0:w1], ALU.mult, ALU.add)\
                        .then_inc(LS, 1)
                    n += 1
            bar(dve, b, 2)
            v.memset(sums[:, 1:TPD], 0.0)
            bar(dve, b, 3)
            bar(dve, b, 4)
            SC = S["scan_step"]
            n_scan = 7
            v.tensor_tensor(work1, work1, work2, ALU.add).then_inc(SC, 1)
            dve.wait_ge(SC, n_scan * b + 1)
            v.tensor_scalar(work2, work1, dirpar[:, 0:1], None, ALU.mult).then_inc(SC, 1)
            dve.wait_ge(SC, n_scan * b + 2)
            for j in range(NCHUNK):
                w = work2[:, 128 * j:128 * j + 128]
                v.tensor_tensor_scan(w, ones[:, :], w, 0.0, ALU.mult, ALU.add)
            bar(dve, b, 5)
            v.tensor_copy(csp[:, :], work2).then_inc(SC, 1)
            bar(dve, b, 6)
            v.scalar_tensor_tensor(work2, csp[:, :], const[:, C_GE1:C_GE1 + 1], work2, ALU.mult, ALU.add)\
                .then_inc(SC, 1)
            dve.wait_ge(SC, n_scan * b + 4)
            v.tensor_copy(csp[:, :], work2).then_inc(SC, 1)
            dve.wait_ge(SC, n_scan * b + 5)
            v.scalar_tensor_tensor(work2, csp[:, :], const[:, C_GE2:C_GE2 + 1], work2, ALU.mult, ALU.add)\
                .then_inc(SC, 1)
            dve.wait_ge(SC, n_scan * b + 6)
            v.tensor_copy(csp[:, :], work2).then_inc(SC, 1)
            bar(dve, b, 7)
            bar(dve, b, 8)
            tok = ps[:, :].rearrange("p (j d r h) -> p j d r h", j=NCHUNK, d=DIRS, r=REP)
            for d in range(DIRS):
                v.tensor_copy(tab_view(dt_tok)[:, d], tok[:, :, d, 0, :])
            bar(dve, b, 9)
            bar(dve, b, 10)
            bar(dve, b, 11)
            v.tensor_tensor(wdt_tok[:, :], ps[:, 0:1024], wdt_tok[:, :], ALU.subtract)
            bar(dve, b, 12)
            bar(dve, b, 13)
            v.tensor_tensor(wdt_tok[:, :], wdt_tok[:, :], dt_tok[:, :], ALU.mult)
            v.memset(tab_view(ecs_tok)[:, :, 0, :], 0.0)
            v.memset(tab_view(dec_bc)[:, :, 0, :], 0.0)
            v.memset(raw[:, :, 0:3], 0.0)
            bar(dve, b, 14)

        def dve_body(dve, b, t):
            v = nc.vector
            i = t + 1
            for c in range(CPT):
                if c == 1 and alive(i - 1):
                    gate_z(dve, b, i - 1, 1)
                if c < XBLK and alive(i):
                    n = XBLK * tile_no(b, i) + c
                    dve.wait_ge(S["xbc_evac"], n + 1)
                    if not first(i):
                        dve.wait_ge(S["conv_done"], n - 2)
                    for k in range(TAPS):
                        w = taps[:, bass.ds(i // TPD * XBLK * TAPS + c * TAPS + k, 1)]
                        if k == 0:
                            v.tensor_scalar(conv[:, c, :], raw[:, c, 0:TILE], w, None, ALU.mult)\
                                .then_inc(S["tap_done"], 1)
                        else:
                            dve.wait_ge(S["tap_done"], TAPS * n + k)
                            v.scalar_tensor_tensor(conv[:, c, :], raw[:, c, k:k + TILE], w, conv[:, c, :],
                                                   ALU.mult, ALU.add).then_inc(S["tap_done"], 1)
                    v.tensor_scalar(raw[:, c, 0:3], raw[:, c, TILE:TILE + 3],
                                    const[:, bass.ds(C_FLAG + i + 1, 1)], None, ALU.mult)\
                        .then_inc(S["conv_done"], 1)
                if c == 3:
                    for cc in range(3):
                        silu(dve, b, i, cc)
                tb, cb = lagged(t, c, 1)
                if alive(tb):
                    k = chunk_no(b, tb, cb)
                    dve.wait_ge(S["st_ready"], k + 1)
                    dve.wait_ge(S["sdec_ready"], k + 1)
                    earlier(dve, "b_done", b, tb, cb, 1)
                    v.tensor_tensor(buf(st, cb + 1, INNER), ps[0:64, 512 * B_S:512 * B_S + INNER], st_dec[:, :],
                                    ALU.add).then_inc(S["s_upd"], 1)
                if alive(t):
                    k = chunk_no(b, t, c)
                    dve.wait_ge(S["l_ready"], k + 1)
                    earlier(dve, "b_done", b, t, c, 2)
                    v.tensor_tensor(mix[:, c % 2], decay[:, c % 2],
                                    buf(xbg, c, 448)[:, 320:448].unsqueeze(1).broadcast_to([128, HEADS, CHUNK]),
                                    ALU.mult).then_inc(S["m_ready"], 1)
                if alive(tb):
                    k = chunk_no(b, tb, cb)
                    earlier(dve, "yg_ready", b, tb, cb, 2)
                    dve.wait_ge(S["b_done"], k + 1)
                    earlier(dve, "ysum_done", b, tb, cb, 1)
                    v.tensor_tensor(by_head(y1[:, :]), by_head(bank(B_Y, 256, 512)), table(ecs_tok, tb, cb),
                                    ALU.mult).then_inc(S["y1_done"], 1)
                    dve.wait_ge(S["y1_done"], k + 1)
                    v.tensor_tensor(buf(y2, cb, INNER), bank(B_Y, 0, 256), y1[:, :], ALU.add)\
                        .then_inc(S["ysum_done"], 1)
                if c == 3:
                    silu(dve, b, i, 3)
                    if alive(i):
                        gate_z(dve, b, i, 0)

        def gate_z(dve, b, i, pair):
            n = tile_no(b, i)
            dve.wait_ge(S["thz_ready"], 2 * n + pair + 1)
            if not first(i):
                dve.wait_ge(S["yg_ready"], CPT * n - CPT + 2 * pair + 2)
            nc.vector.scalar_tensor_tensor(gate[:, 512 * pair:512 * pair + 512], thz[:, :], 1.0, bank(B_P),
                                           ALU.add, ALU.mult).then_inc(S["z_evac"], 1)

        def silu(dve, b, i, c):
            if not alive(i):
                return
            v = nc.vector
            dve.wait_ge(S["tanh_done"], 3 * tile_no(b, i) + 3)
            if not first(i):
                k = chunk_no(b, i, c) - CPT
                dve.wait_ge(S["tbank_ready"], k + 1)
                dve.wait_ge(S["x_ready"], k + 1)
            cols = slice(128 * c, 128 * c + 128)
            v.scalar_tensor_tensor(xs_v[:, c], tanh[:, :, cols], 1.0, conv[:, :, cols], ALU.add, ALU.mult)
            v.scalar_tensor_tensor(cs_[:, cols], tanh[64:128, 2, cols], 1.0, conv[64:128, 2, cols],
                                   ALU.add, ALU.mult).then_inc(S["silu_done"], 1)

        def order_parts(d):
            im = lambda x: x.rearrange("p (h w) -> p h w", w=64)
            s = seq[:, d, :].rearrange("p (a b) -> p a b", b=64)
            if d == 0:
                return [(lambda x: im(x), s)]
            if d == 1:
                return [(lambda x: im(x), s.rearrange("p w h -> p h w"))]
            if d == 2:
                return [(lambda x: im(x)[:, 0::2, :], s[:, 0::2, :]),
                        (lambda x: im(x)[:, 1::2, :], s[:, 1::2, ::-1])]
            return [(lambda x: im(x)[:, :, 0::2].rearrange("p h w -> p w h"), s[:, 0::2, :]),
                    (lambda x: im(x)[:, :, 1::2].rearrange("p h w -> p w h"), s[:, 1::2, ::-1])]

        def dve_post(dve, b):
            v = nc.vector
            bar(dve, b, 15)
            P_ = S["post_step"]
            v.reduce_sum(small[:, 0:5], sums[:, :].rearrange("p (k t) -> p k t", k=BRANCHES), AX_X).then_inc(P_, 1)
            step(dve, b, 2)
            w1 = vbc[:, V_W1:V_W1 + 10].rearrange("p (i j) -> p j i", j=2)
            desc = bank(4, 0, BRANCHES).unsqueeze(1).broadcast_to([128, 2, BRANCHES])
            v.scalar_tensor_tensor(small[:, 44:54].rearrange("p (j i) -> p j i", j=2), desc, 1.0 / (CH * PIX), w1,
                                   ALU.mult, ALU.mult).then_inc(P_, 1)
            step(dve, b, 3)
            SS = S["fuse_step"]
            n_fuse = 8
            v.reduce_sum(small[:, 6:8], small[:, 44:54].rearrange("p (j i) -> p j i", j=2), AX_X).then_inc(SS, 1)
            dve.wait_ge(SS, n_fuse * b + 1)
            v.tensor_tensor(small[:, 8:10], small[:, 6:8], vbc[:, V_B1:V_B1 + 2], ALU.add).then_inc(P_, 1)
            step(dve, b, 5)
            w2 = vbc[:, V_W2:V_W2 + 10].rearrange("p (j i) -> p i j", j=2)
            v.tensor_tensor(small[:, 44:54].rearrange("p (i j) -> p i j", j=2),
                            small[:, 8:10].unsqueeze(1).broadcast_to([128, BRANCHES, 2]), w2, ALU.mult).then_inc(SS, 1)
            dve.wait_ge(SS, n_fuse * b + 2)
            v.reduce_sum(small[:, 54:59], small[:, 44:54].rearrange("p (i j) -> p i j", j=2), AX_X).then_inc(SS, 1)
            dve.wait_ge(SS, n_fuse * b + 3)
            v.tensor_tensor(small[:, 12:17], small[:, 54:59], vbc[:, V_B2:V_B2 + 5], ALU.add).then_inc(P_, 1)
            step(dve, b, 7)
            v.tensor_scalar(small[:, 12:17], small[:, 12:17], 0.5, 0.5, ALU.mult, ALU.add).then_inc(P_, 1)
            stats = gate[:, 0:6 * TPD]
            for q in range(TPD):
                dve.wait_ge(S["proj_evac"], TPD * b + q + 1)
                last = v.bn_stats(stats[:, 6 * q:6 * q + 6], work1[:, 512 * q:512 * q + 512])
            last.then_inc(SS, 1)
            dve.wait_ge(SS, n_fuse * b + 4)
            step(dve, b, 8)
            settle(dve)
            v.bn_aggr(small[:, 20:22], stats).then_inc(P_, 1)
            step(dve, b, 10)
            v.tensor_copy(small[:, 22:23], bank(5, 0, 1)).then_inc(SS, 1)
            dve.wait_ge(SS, n_fuse * b + 5)
            v.tensor_tensor(small[:, 23:24], small[:, 20:21], small[:, 22:23], ALU.subtract).then_inc(P_, 1)
            step(dve, b, 11)
            v.scalar_tensor_tensor(small[:, 24:25], small[:, 23:24], small[:, 23:24], small[:, 21:22],
                                   ALU.mult, ALU.add).then_inc(P_, 1)
            step(dve, b, 13)
            v.tensor_scalar(small[:, 25:26], bank(6, 0, 1), EPS, None, ALU.add).then_inc(SS, 1)
            dve.wait_ge(S["var_done"], (BATCH_CHUNKS + 1) * b + BATCH_CHUNKS + 1)
            v.tensor_tensor(small[:, 28:29], small[:, 26:27], gnp[:, 0:1], ALU.mult).then_inc(SS, 1)
            dve.wait_ge(SS, n_fuse * b + 7)
            v.tensor_tensor(small[:, 27:28], small[:, 28:29], small[:, 22:23], ALU.mult).then_inc(SS, 1)
            dve.wait_ge(SS, n_fuse * b + 8)
            v.tensor_tensor(small[:, 29:30], gnp[:, 1:2], small[:, 27:28], ALU.subtract).then_inc(P_, 1)
            dve.wait_ge(S["x_loaded"], 32 * b + 32)
            FS = S["tap_done_post"]
            n = 0
            v.scalar_tensor_tensor(work2, local[:, :], small[:, 12:13], work2, ALU.mult, ALU.add).then_inc(FS, 1)
            for d in range(DIRS):
                n += 1
                dve.wait_ge(FS, 5 * b + n)
                for pick, src in order_parts(d):
                    last = v.scalar_tensor_tensor(pick(work2), src, small[:, 13 + d:14 + d], pick(work2),
                                                  ALU.mult, ALU.add)
                last.then_inc(FS, 1)
            dve.wait_ge(FS, 5 * b + 5)
            for q in range(4):
                dve.wait_ge(S["stat_step"], 4 * b + q + 1)
                w = slice(1024 * q, 1024 * q + 1024)
                v.tensor_tensor(work2[:, w], work2[:, w], work1[:, w], ALU.add).then_inc(S["part_ready"], 1)
            bar(dve, b, 16)

        S["tap_done_post"] = sem("branch_added")
        BATCH_CHUNKS = TILES * CPT

        def dve_program(dve):
            dve_setup(dve)
            with dve.Fori(0, BATCH) as b:
                dve_prep(dve, b)
                run_tiles(dve, b, dve_body)
                dve_post(dve, b)

        def pool_setup(pool):
            for n in range(SETUP_BARS):
                barrier(pool, n)

        def pool_prep(pool, b):
            g = nc.gpsimd
            bar(pool, b, 0)
            bar(pool, b, 1)
            img = seq[:, 0, :].rearrange("p (h w) -> p h w", w=64)
            for d in (2, 3):
                for pick, dst in order_parts(d):
                    g.tensor_copy(dst, pick(seq[:, 0, :]))
            for n in range(2, 15):
                bar(pool, b, n)

        def pool_body(pool, b, t):
            g = nc.gpsimd
            for c in range(CPT):
                tr, cr = lagged(t, c, 3)
                if alive(tr):
                    k = chunk_no(b, tr, cr)
                    pool.wait_ge(S["ss_ready"], k + 1)
                    earlier(pool, "yr_ready", b, tr, cr, 2)
                    settle(pool)
                    p = cr % 2
                    g.tensor_scalar(small[:, 34 + p:35 + p], small[:, 32 + p:33 + p], 1.0 / INNER, 4 * EPS,
                                    ALU.mult, ALU.add).then_inc(S["var_done"], 1)
                    pool.wait_ge(S["var_done"], k + b + 1)
                    g.tensor_tensor(small[:, 36 + p:37 + p], small[:, 34 + p:35 + p], small[:, 60:61], ALU.pow)\
                        .then_inc(S["r_ready"], 1)
                ty, cy = lagged(t, c, 2)
                if alive(ty):
                    k = chunk_no(b, ty, cy)
                    pool.wait_ge(S["ysum_done"], k + 1)
                    pool.wait_ge(S["x_ready"], k + 1)
                    g.tensor_tensor(buf(y2, cy, INNER), buf(y2, cy, INNER), buf(xd, cy, INNER), ALU.add)\
                        .then_inc(S["y3_done"], 1)
                    pool.wait_ge(S["y3_done"], k + 1)
                    pool.wait_ge(S["z_evac"], 2 * tile_no(b, ty) + cy // 2 + 1)
                    earlier(pool, "yr_ready", b, ty, cy, 2)
                    g.tensor_tensor(buf(yg, cy, INNER), buf(y2, cy, INNER), gate[:, INNER * cy:INNER * cy + INNER], ALU.mult)\
                        .then_inc(S["yg_ready"], 1)
                if alive(t):
                    k = chunk_no(b, t, c)
                    pool.wait_ge(S["xbg_ready"], k + 1)
                    earlier(pool, "b_done", b, t, c, 2)
                    pool.wait_ge(S["silu_done"], k + 1)
                    settle(pool)
                    x_ = by_head(buf(xbg, c, 448)[:, 0:256])
                    g.tensor_copy(buf(c_use, c, CHUNK), cs_[:, 128 * c:128 * c + 128])
                    g.tensor_tensor(by_head(buf(xdt, c, INNER)), x_, table(dt_tok, t, c), ALU.mult)
                    g.tensor_tensor(by_head(buf(xw, c, INNER)), x_, table(wdt_tok, t, c), ALU.mult)
                    dp = heads(vbc[:, bass.ds(V_DP + t // TPD * HEADS, HEADS)])
                    earlier(pool, "yg_ready", b, t, c, 2)
                    settle(pool)
                    g.tensor_tensor(by_head(buf(xd, c, INNER)), x_, dp, ALU.mult).then_inc(S["x_ready"], 1)
                    earlier(pool, "s_upd", b, t, c, 1)
                    settle(pool)
                    g.tensor_tensor(by_head(st_dec[:, :]), by_head(buf(st, c, INNER)), table(dec_bc, t, c, 64),
                                    ALU.mult).then_inc(S["sdec_ready"], 1)

        def pool_post(pool, b):
            bar(pool, b, 15)
            pool.wait_ge(S["fuse_step"], 8 * b + 6)
            nc.gpsimd.tensor_tensor(small[:, 26:27], small[:, 25:26], small[:, 60:61], ALU.pow)\
                .then_inc(S["var_done"], 1)
            bar(pool, b, 16)

        def pool_program(pool):
            pool_setup(pool)
            with pool.Fori(0, BATCH) as b:
                pool_prep(pool, b)
                run_tiles(pool, b, pool_body)
                pool_post(pool, b)

        block = ctx.enter_context(nc.Block())

        @block.sync
        def _(sp):
            sp_program(sp)

        @block.tensor
        def _(pe):
            pe_program(pe)

        @block.scalar
        def _(act):
            act_program(act)

        @block.vector
        def _(dve):
            dve_program(dve)

        @block.gpsimd
        def _(pool):
            pool_program(pool)


_INS = ["x", "L0_conv_pos_proj_w", "L0_conv_local_w", "L0_conv_W_in", "L0_conv_conv_w", "L0_conv_A_log",
        "L0_conv_dt_bias", "L0_conv_Dp", "L0_conv_norm_w", "L0_conv_W_out", "L0_conv_se_w1", "L0_conv_se_b1",
        "L0_conv_se_w2", "L0_conv_se_b2", "L0_conv_proj_w", "L0_conv_gn_gamma", "L0_conv_gn_beta"]


def kernel(**inputs):
    import concourse.bacc as _bacc
    from concourse.bass_utils import run_bass_kernel_spmd as _run

    nc = _bacc.Bacc("TRN2", target_bir_lowering=False, num_devices=1)
    arrays, aps = {}, {}
    for name in _INS:
        arr = np.ascontiguousarray(inputs[name])
        arrays[f"in_{name}_dram"] = arr
        aps[name.replace("L0_conv_", "")] = nc.dram_tensor(
            f"in_{name}_dram", arr.shape, mybir.dt.from_np(arr.dtype), kind="ExternalInput").ap()
    arrays["shape_const_dram"] = shape_constants()
    aps["shape_const"] = nc.dram_tensor("shape_const_dram", (128, C_COLS), F32, kind="ExternalInput").ap()
    out = nc.dram_tensor("out_0_dram", (BATCH, CH, HEIGHT, WIDTH), F32, kind="ExternalOutput").ap()
    build(nc, aps, out)
    r = _run(nc, [arrays], core_ids=[0])
    return r.results[0]["out_0_dram"]
```

```python
from contextlib import ExitStack

import numpy as np
import concourse.bass as bass
from concourse import mybir

F32 = mybir.dt.float32
BF16 = mybir.dt.bfloat16
ALU = mybir.AluOpType
ACT = mybir.ActivationFunctionType
AX_X = mybir.AxisListType.X

BATCH, CH, HEIGHT, WIDTH = 8, 128, 64, 64
PIX = HEIGHT * WIDTH
DIRS = 4
STATE = 64
HEADS, HEAD = 8, 32
INNER = HEADS * HEAD
CONV = INNER + 2 * STATE
XBLK = CONV // 128
TAPS = 4
CHUNK = 128
TILE = 512
CPT = TILE // CHUNK
TPD = PIX // TILE
TILES = DIRS * TPD
NCHUNK = PIX // CHUNK
BRANCHES = 5
GROUP = CH // 8
REP = 4
SPLIT = 3
EPS = 1e-5

C_IDENT, C_TRI, C_LAST, C_GROUP, C_POS = 0, 128, 256, 384, 512
C_SEL, C_NEG, C_FLAG, C_GE1, C_GE2, C_GE0 = 576, 608, 640, 680, 681, 682
C_COLS = 683
V_ALOG, V_DTB, V_DP, V_W1, V_B1, V_W2, V_B2 = 0, 32, 64, 96, 106, 108, 118
V_COLS = 123


def shape_constants():
    t = np.zeros((128, C_COLS), np.float32)
    i = np.arange(128)
    t[:, C_IDENT:C_IDENT + 128] = np.eye(128)
    t[:, C_TRI:C_TRI + 128] = -1e30 * (i[None, :] < i[:, None])
    t[127, C_LAST:C_LAST + 128] = 1.0
    t[:, C_GROUP:C_GROUP + 128] = (i[:, None] // GROUP == i[None, :] // GROUP) / GROUP
    half = CH // 2
    freq = 10000.0 ** (np.arange(0, half, 2, dtype=np.float32) / half)
    ph = np.arange(HEIGHT, dtype=np.float32)[:, None] / freq
    emb = np.stack([np.sin(ph), np.cos(ph)], 2).reshape(HEIGHT, -1).T
    t[0:64, C_POS:C_POS + 64] = emb
    t[64:128, C_POS:C_POS + 64] = emb
    row_dir, row_rep, row_head = i // 32, i // 8 % 4, i % 8
    for d in range(DIRS):
        for h in range(HEADS):
            own = (row_dir == d) & (row_head == h) & (row_rep < SPLIT)
            t[:, C_SEL + 8 * d + h] = own
            t[:, C_NEG + 8 * d + h] = -1.0 * own
    t[:, C_FLAG:C_FLAG + 40] = np.arange(40) % TPD != 0
    t[:, C_GE0] = -1.0 * (row_rep < SPLIT)
    t[:, C_GE1] = -1.0 * (row_rep >= 1)
    t[:, C_GE2] = -1.0 * (row_rep >= 2)
    return t


def build(nc, a, out):
    ctx = ExitStack()
    with ctx:
        def sb(name, shape, dt=F32):
            return ctx.enter_context(nc.sbuf_tensor(name, shape, dt))

        def sem(name):
            return ctx.enter_context(nc.semaphore(name))

        useq = sb("useq", [128, DIRS * PIX])
        local = sb("local", [128, PIX])
        arena1 = sb("arena1", [128, PIX])
        arena2 = sb("arena2", [128, 3 * (3 + TILE) + 6 * TILE])
        csp = sb("csp", [128, PIX], BF16)
        sel = sb("sel", [128, DIRS * HEADS], BF16)
        ident_b = sb("ident_b", [128, 128], BF16)
        later = sb("later", [128, 128], BF16)
        neg = sb("neg", [128, DIRS * HEADS], BF16)
        const = sb("const", [128, C_COLS])
        vbc = sb("vbc", [128, V_COLS])
        ones = sb("ones", [128, 128])
        dt_tok = sb("dt_tok", [128, DIRS * NCHUNK * HEADS])
        wdt_tok = sb("wdt_tok", [128, DIRS * NCHUNK * HEADS])
        dec_bc = sb("dec_bc", [128, DIRS * NCHUNK * 4])
        wz = sb("wz", [128, INNER])
        sel_e = sb("sel_e", [128, DIRS * INNER], BF16)
        wo_all = sb("wo_all", [128, DIRS * 2 * CH])
        wdt = sb("wdt", [128, DIRS * 32])
        wx = sb("wx", [128, CONV])
        wo = sb("wo", [128, 2 * CH])
        taps = sb("taps", [128, DIRS * XBLK * TAPS])
        lw = sb("lw", [128, 9])
        pw_t = sb("pw_t", [128, BRANCHES * CH])
        posw_t = sb("posw_t", [128, CH])
        pos = sb("pos", [128, 2 * 64])
        gnp = sb("gnp", [128, 2])
        nw_t = sb("nw_t", [128, 8])
        d_col = sb("d_col", [128, DIRS * 2])
        dirpar = sb("dirpar", [128, 2])
        sums = sb("sums", [128, BRANCHES * TPD])
        small = sb("small", [128, 64])
        xs = sb("xs", [128, 2 * CPT * CONV])
        c_low = sb("c_low", [64, 2 * CPT * CHUNK])
        xbg = sb("xbg", [128, 2 * 448])
        xdt = sb("xdt", [128, 2 * INNER])
        xw = sb("xw", [128, 2 * INNER])
        xd = sb("xd", [128, 2 * INNER])
        thz = sb("thz", [128, TILE])
        gate = sb("gate", [128, 2 * TILE])
        ecs = sb("ecs", [128, 2 * TILE])
        y1 = sb("y1", [128, INNER])
        y2 = sb("y2", [128, 2 * INNER])
        ygs = [sb(f"yg{n}", [128, 2 * TILE]) for n in range(2)]
        sq = sb("sq", [128, 2 * TILE])
        var = sb("var", [128, CPT])
        rms = sb("rms", [128, CPT])
        half_pow = sb("half_pow", [128, CPT])
        rbc = sb("rbc", [128, TILE])
        st = sb("st", [128, 2 * CHUNK])
        st_dec = sb("st_dec", [128, CHUNK])
        ps = ctx.enter_context(nc.psum_tensor("ps", [128, 8 * 512], F32))

        def bank(n, lo=0, hi=512):
            return ps[:, 512 * n + lo:512 * n + hi]

        B_PX, B_T, B_D, B_Y, B_PZ, B_S = 0, 1, 2, 4, 6, 7

        ident = const[:, C_IDENT:C_IDENT + 128]
        decay = arena1[:, 0:2048].rearrange("p (b h t) -> p b h t", b=2, h=HEADS)
        mix = arena1[:, 2048:4096].rearrange("p (b h t) -> p b h t", b=2, h=HEADS)
        RAW = 3 + TILE
        raw = arena2[:, 0:3 * RAW].rearrange("p (j t) -> p j t", j=XBLK)
        conv = arena2[:, 3 * RAW:3 * RAW + 3 * TILE].rearrange("p (j t) -> p j t", j=XBLK)
        tanh = arena2[:, 3 * RAW + 3 * TILE:3 * RAW + 6 * TILE].rearrange("p (j t) -> p j t", j=XBLK)
        y_banks = ps[:, 512 * B_Y:512 * B_Y + 1024].rearrange("p (m t) -> p m t", m=2)
        seq = useq[:, :].rearrange("p (d n) -> p d n", d=DIRS)
        work1, work2 = arena1[:, :], arena2[:, 0:PIX]
        vrow = arena2[0:1, 128:128 + V_COLS]

        S = {n: sem(n) for n in (
            "phase", "loaded", "setup_step", "x_loaded", "prep_step", "local_step", "scan_step",
            "post_step", "proj_ready", "proj_evac", "fuse_step", "stored", "part_ready",
            "wx_loaded", "wz_loaded", "wo_loaded", "xbc_ready", "z_ready", "e_ready",
            "xbc_evac", "thz_ready", "gate_done", "ecs_ready", "tap_done", "conv_done", "tanh_done",
            "silu_done", "tbank_ready", "d_ready", "xbg_ready", "l_ready", "x_ready", "m_ready",
            "st_ready", "sdec_ready", "s_upd", "b_done", "y1_done", "ysum_done", "y3_done", "yg_ready",
            "sq_ready", "ss_ready", "ss_evac", "var_done", "r_ready", "rbc_mm", "rbc_ready", "out_ready",
            "o_evac", "stat_step", "wdt_step", "settled")}

        SETUP_BARS, BATCH_BARS = 7, 17

        def settle(eng):
            eng.sem_inc(S["settled"], 1)

        def barrier(eng, count):
            eng.drain().then_inc(S["phase"], 1)
            eng.wait_ge(S["phase"], 5 * (count + 1))
            settle(eng)

        def bar(eng, b, n):
            barrier(eng, SETUP_BARS + b * BATCH_BARS + n)

        def alive(t):
            return not isinstance(t, int) or 0 <= t < TILES

        def first(t):
            return isinstance(t, int) and t == 0

        def lagged(t, c, lag):
            return (t, c - lag) if c >= lag else (t - 1, c - lag + CPT)

        def tile_no(b, t):
            return b * TILES + t

        def chunk_no(b, t, c):
            return (b * TILES + t) * CPT + c

        def earlier(eng, name, b, t, c, lag):
            if not (first(t) and c < lag):
                eng.wait_ge(S[name], chunk_no(b, t, c) - lag + 1)

        def heads(ap, n=HEAD):
            p, h = ap.shape
            return ap.unsqueeze(2).broadcast_to([p, h, n])

        def by_head(ap):
            return ap.rearrange("p (h d) -> p h d", h=HEADS)

        def table(tab, t, c, n=HEADS):
            ap = tab[:, bass.ds((t * CPT + c) * n, n)]
            return heads(ap)

        P_USES = {B_PX: (("xbc", 1, 0), ("xbc", 2, 0), ("xbc", 0, 1), ("out", 0, -2)),
                  B_PZ: (("e", 1, -1), ("ss", 0, -2), ("z", 1, -1), ("e", 0, 0), ("rbc", 0, -2), ("z", 0, 0))}
        READ_OUT = {"xbc": ("xbc_evac", XBLK), "rbc": ("rbc_ready", 1), "ss": ("ss_evac", 1), "out": ("o_evac", 1),
                    "z": ("gate_done", 2), "e": ("ecs_ready", 2)}

        def p_wait(pe, b, i, kind, part=0):
            uses = [u for us in P_USES.values() if (kind, part) in [x[:2] for x in us] for u in us]
            at = [u[:2] for u in uses].index((kind, part))
            for back in range(1, 4 * len(uses)):
                k, body = (at - back) % len(uses), i + (at - back) // len(uses)
                name, part_, lag = uses[k]
                if alive(body + lag):
                    evac, per = READ_OUT[name]
                    pe.wait_ge(S[evac], per * tile_no(b, body + lag) + part_ + 1)
                    return

        RING = 2 * CPT

        def slot(odd, c, lag=0):
            return (CPT * odd + c - lag) % RING

        def xs_of(s):
            return xs[:, s * CONV:s * CONV + CONV].rearrange("p (j t) -> p j t", j=XBLK)

        def c_of(s):
            return c_low[:, s * CHUNK:s * CHUNK + CHUNK]

        def pair_of(ap, c):
            return ap[:, TILE * (c // 2):TILE * (c // 2) + TILE].rearrange("p (m t) -> p m t", m=2)[
                :, :, CHUNK * (c % 2):CHUNK * (c % 2) + CHUNK]

        def two(ap):
            return ap.rearrange("p (m t) -> p m t", m=2)

        def buf(t_, c, w):
            return t_[:, (c % 2) * w:(c % 2) * w + w]

        def run_tiles(eng, b, body):
            for t in range(-2, 4):
                body(eng, b, t, t % 2)
            with eng.Fori(2, TILES // 2 - 1) as u:
                body(eng, b, u * 2, 0)
                body(eng, b, u * 2 + 1, 1)
            for t in range(TILES - 2, TILES + 2):
                body(eng, b, t, t % 2)

        def sp_setup(sp):
            L = S["loaded"]
            sp.dma_start(const[:, :], a["shape_const"]).then_inc(L, 16)
            for name, at, n in (("A_log", V_ALOG, 32), ("dt_bias", V_DTB, 32), ("Dp", V_DP, 32)):
                sp.dma_start(vrow[0:1, at:at + n], a[name].rearrange("(o d) h -> o (d h)", o=1)).then_inc(L, 16)
            for name, at, n in (("se_w1", V_W1, 10), ("se_w2", V_W2, 10)):
                sp.dma_start(vrow[0:1, at:at + n], a[name].rearrange("(o d) h -> o (d h)", o=1)).then_inc(L, 16)
            for name, at, n in (("se_b1", V_B1, 2), ("se_b2", V_B2, 5)):
                sp.dma_start(vrow[0:1, at:at + n], a[name].rearrange("(o d) -> o d", o=1)).then_inc(L, 16)
            w_in = a["W_in"].rearrange("d c n -> c d n")
            sp.dma_start(small[:, 0:32].rearrange("p (d n) -> p d n", d=DIRS),
                         w_in[:, :, INNER + CONV:INNER + CONV + HEADS]).then_inc(L, 16)
            sp.dma_start(wo_all[:, :].rearrange("p (d m o) -> p d m o", d=DIRS, m=2),
                         a["W_out"].rearrange("d (m k) o -> k d m o", m=2)).then_inc(L, 16)
            sp.dma_start(lw[:, :], a["local_w"].rearrange("c u i j -> c (u i j)")).then_inc(L, 16)
            sp.dma_start(gnp[:, 0:1], a["gn_gamma"].rearrange("(c o) -> c o", o=1)).then_inc(L, 16)
            sp.dma_start(gnp[:, 1:2], a["gn_beta"].rearrange("(c o) -> c o", o=1)).then_inc(L, 16)
            sp.dma_start(arena1[:, 0:640], a["proj_w"]).then_inc(L, 16)
            sp.dma_start(arena1[:, 640:768], a["pos_proj_w"]).then_inc(L, 16)
            sp.dma_start(arena1[0:8, 768:896], a["norm_w"].rearrange("d (m k) -> (d m) k", m=2)).then_inc(L, 16)
            sp.dma_start(arena1[0:16, 1024:1024 + CONV], a["conv_w"].rearrange("d k c -> (d k) c")).then_inc(L, 16)
            sp.wait_ge(L, 16 * 17)
            for n in range(SETUP_BARS):
                barrier(sp, n)

        def sp_body(sp, b, t, odd):
            i = t + 1
            if alive(t - 1):
                if not first(t - 1):
                    sp.wait_ge(S["out_ready"], tile_no(b, t - 1))
                    settle(sp)
                sp.dma_start(wo[:, :], wo_all[:, bass.ds((t - 1) // TPD * 2 * CH, 2 * CH)]).then_inc(S["wo_loaded"], 16)
            if alive(i + 1):
                if not first(i + 1):
                    sp.wait_ge(S["xbc_ready"], 3 * tile_no(b, i + 1))
                    settle(sp)
                load_w(sp, i + 1, wx, INNER, INNER + CONV, "wx_loaded")
            if alive(i):
                if not first(i):
                    sp.wait_ge(S["z_ready"], 2 * tile_no(b, i))
                    settle(sp)
                load_w(sp, i, wz, 0, INNER, "wz_loaded")

        def load_w(sp, i, dst, lo, hi, name):
            d = i // TPD
            w = a["W_in"][d, :, lo:hi] if isinstance(d, int) else \
                a["W_in"][bass.ds(d, 1), :, lo:hi].rearrange("d c n -> c (d n)")
            sp.dma_start(dst[:, :], w).then_inc(S[name], 16)

        def sp_program(sp):
            sp_setup(sp)
            with sp.Fori(0, BATCH) as b:
                x_img = a["x"][bass.ds(b, 1)].rearrange("b c h w -> c (b h w)")
                sp.dma_start(seq[:, 0, :], x_img).then_inc(S["x_loaded"], 16)
                sp.wait_ge(S["x_loaded"], 32 * b + 16)
                settle(sp)
                for n in range(15):
                    bar(sp, b, n)
                run_tiles(sp, b, sp_body)
                bar(sp, b, 15)
                sp.dma_start(work2, x_img).then_inc(S["x_loaded"], 16)
                sp.wait_ge(S["x_loaded"], 32 * b + 32)
                out_img = out[bass.ds(b, 1)].rearrange("b c h w -> c (b h w)")
                for q in range(4):
                    sp.wait_ge(S["part_ready"], 4 * b + q + 1)
                    sp.dma_start(out_img[:, q * 1024:(q + 1) * 1024], work2[:, q * 1024:(q + 1) * 1024])\
                        .then_inc(S["stored"], 16)
                sp.wait_ge(S["stored"], 64 * b + 64)
                settle(sp)
                bar(sp, b, 16)

        def pe_setup(pe):
            barrier(pe, 0)
            mm = nc.tensor
            for k in range(BRANCHES):
                mm.transpose(bank(k, 0, 128), arena1[:, 128 * k:128 * k + 128], ident)
            mm.transpose(bank(5, 0, 128), arena1[:, 640:768], ident)
            mm.transpose(bank(6, 0, 8), arena1[0:8, 768:896], ident[0:8, 0:8])
            for j in range(XBLK):
                mm.transpose(bank(6, 16 + 16 * j, 32 + 16 * j), arena1[0:16, 1024 + 128 * j:1152 + 128 * j],
                             ident[0:16, 0:16])
            mm.matmul(bank(7, 0, V_COLS), ones[0:1, :], vrow[0:1, :], start=True, stop=True)
            barrier(pe, 1)
            barrier(pe, 2)
            mm.matmul(bank(0, 0, 64), posw_t[0:64, :], const[0:64, C_POS:C_POS + 64], start=True, stop=True)
            mm.matmul(bank(1, 0, 64), posw_t[64:128, :], const[64:128, C_POS:C_POS + 64], start=True, stop=True)
            for n in range(3, SETUP_BARS):
                barrier(pe, n)

        def pe_prep(pe, b):
            mm = nc.tensor
            bar(pe, b, 0)
            bar(pe, b, 1)
            bar(pe, b, 2)
            for q in range(TPD):
                for d in range(DIRS):
                    mm.matmul(ps[32 * d:32 * d + 32, 512 * q:512 * q + 512], wdt[:, 32 * d:32 * d + 32],
                              seq[:, d, 512 * q:512 * q + 512], start=True, stop=True)
            bar(pe, b, 3)
            bar(pe, b, 4)
            bar(pe, b, 5)
            for j in range(NCHUNK):
                mm.transpose(ps[:, 128 * j:128 * j + 128], work2[:, 128 * j:128 * j + 128], ident)
            bar(pe, b, 6)
            bar(pe, b, 7)
            for j in range(NCHUNK):
                mm.transpose(ps[:, 128 * j:128 * j + 128], work1[:, 128 * j:128 * j + 128], ident)
            bar(pe, b, 8)
            bar(pe, b, 9)
            for q in range(2):
                mm.matmul(bank(q), const[:, C_LAST:C_LAST + 128], wdt_tok[:, 512 * q:512 * q + 512],
                          start=True, stop=True)
            for n in range(10, 15):
                bar(pe, b, n)

        def pe_body(pe, b, t, odd):
            mm = nc.tensor
            i = t + 1
            for c in range(CPT):
                if alive(t):
                    chunk_head(pe, b, t, c, slot(odd, c))
                if c == 3:
                    spread_cs(pe, b, i, i, 0)
                tb, cb = lagged(t, c, 1)
                if alive(tb):
                    chunk_tail(pe, b, tb, cb, slot(odd, c, 1))
                if c < 2:
                    project_xbc(pe, b, i, c + 1)
                if c == 1:
                    spread_cs(pe, b, i, t, 1)
                if c == 2:
                    if alive(t - 1):
                        n = tile_no(b, t - 1)
                        pe.wait_ge(S["sq_ready"], CPT * n + CPT)
                        p_wait(pe, b, i, "ss")
                        for j in range(CPT):
                            for m in range(2):
                                last = mm.matmul(bank(B_PZ, j, j + 1),
                                                 sq[:, TILE * m + CHUNK * j:TILE * m + CHUNK * j + CHUNK],
                                                 ones[:, 0:1], start=(m == 0), stop=(m == 1))
                        last.then_inc(S["ss_ready"], 1)
                    project_xbc(pe, b, i + 1, 0)
                    project_z(pe, b, i, t, 1)
                if c == 3:
                    if alive(t - 1):
                        n = tile_no(b, t - 1)
                        pe.wait_ge(S["r_ready"], n + 1)
                        p_wait(pe, b, i, "rbc")
                        for j in range(CPT):
                            last = mm.matmul(bank(B_PZ, CHUNK * j, CHUNK * j + CHUNK),
                                             rms[:, j:j + 1].broadcast_to([128, 128]), ident,
                                             start=True, stop=True)
                        last.then_inc(S["rbc_mm"], 1)
                        pe.wait_ge(S["wo_loaded"], 16 * n + 16)
                        p_wait(pe, b, i, "out")
                        for m in range(2):
                            last = mm.matmul(bank(B_PX), wo[:, 128 * m:128 * m + 128], ygs[1 - odd][:, TILE * m:TILE * m + TILE],
                                             start=(m == 0), stop=(m == 1))
                        last.then_inc(S["out_ready"], 1)
                    project_z(pe, b, i, i, 0)

        def project_xbc(pe, b, i, j):
            if not alive(i):
                return
            n = tile_no(b, i)
            if j == 0:
                pe.wait_ge(S["wx_loaded"], 16 * n + 16)
            p_wait(pe, b, i - 1 if j == 0 else i, "xbc", j)
            nc.tensor.matmul(bank(B_PX), wx[:, 128 * j:128 * j + 128], useq[:, bass.ds(i * TILE, TILE)],
                             start=True, stop=True).then_inc(S["xbc_ready"], 1)

        def project_z(pe, b, i, tile, pair):
            if not alive(tile):
                return
            n = tile_no(b, tile)
            if pair == 0:
                pe.wait_ge(S["wz_loaded"], 16 * n + 16)
            p_wait(pe, b, i, "z", pair)
            for m in range(2):
                last = nc.tensor.matmul(bank(B_PZ, 256 * m, 256 * m + 256), wz[:, 128 * m:128 * m + 128],
                                        useq[:, bass.ds(tile * TILE + 256 * pair, 256)], start=True, stop=True)
            last.then_inc(S["z_ready"], 1)

        def spread_cs(pe, b, i, tile, pair):
            if not alive(tile):
                return
            p_wait(pe, b, i, "e", pair)
            d = tile // TPD
            for m in range(2):
                last = nc.tensor.matmul(bank(B_PZ, 256 * m, 256 * m + 256),
                                        sel_e[:, bass.ds(d * INNER + 128 * m, 128)],
                                        csp[:, bass.ds(tile % TPD * TILE + 256 * pair, 256)],
                                        start=True, stop=True)
            last.then_inc(S["e_ready"], 1)

        def chunk_head(pe, b, t, c, at):
            mm = nc.tensor
            k = chunk_no(b, t, c)
            pe.wait_ge(S["silu_done"], k + 1)
            earlier(pe, "xbg_ready", b, t, c, 1)
            for j in range(2):
                mm.transpose(bank(B_T, 128 * j, 128 * j + 128), xs_of(at)[:, j, :], ident)
            mm.transpose(bank(B_T, 256, 320), xs_of(at)[0:64, 2, :], ident[0:64, 0:64])
            mm.matmul(bank(B_T, 320, 448), xs_of(at)[0:64, 2, :], c_of(at),
                      start=True, stop=True).then_inc(S["tbank_ready"], 1)
            earlier(pe, "l_ready", b, t, c, 1)
            d = t // TPD
            cols = csp[:, bass.ds(t % TPD * TILE + c * CHUNK, CHUNK)]
            for q in range(2):
                for h in range(4):
                    mm.matmul(bank(B_D + q, 128 * h, 128 * h + 128),
                              sel[:, bass.ds(d * HEADS + 4 * q + h, 1)].broadcast_to([128, 128]), cols,
                              start=(h == 0), stop=False, skip_group_check=True)
                mm.matmul(bank(B_D + q), ident_b[:, :], later[:, :].unsqueeze(1).broadcast_to([128, 4, 128]),
                          start=False, stop=False, skip_group_check=True)
                last = mm.matmul(bank(B_D + q), cols,
                                 neg[:, bass.ds(d * HEADS + 4 * q, 4)].unsqueeze(2).broadcast_to([128, 4, 128]),
                                 start=False, stop=True, skip_group_check=True)
            last.then_inc(S["d_ready"], 1)

        def chunk_tail(pe, b, t, c, at):
            mm = nc.tensor
            k = chunk_no(b, t, c)
            pe.wait_ge(S["x_ready"], k + 1)
            earlier(pe, "s_upd", b, t, c, 1)
            for m in range(2):
                last = mm.matmul(bank(B_S, 0, CHUNK)[64 * m:64 * m + 64],
                                 buf(xbg, c, 448)[:, 256:320], buf(xw, c, INNER)[:, 128 * m:128 * m + 128],
                                 start=True, stop=True)
            last.then_inc(S["st_ready"], 1)
            pe.wait_ge(S["m_ready"], k + 1)
            earlier(pe, "ysum_done", b, t, c, 1)
            for h in range(HEADS):
                q = h % 4
                mm.matmul(ps[32 * q:32 * q + 32, 512 * (B_Y + h // 4):512 * (B_Y + h // 4) + CHUNK],
                          buf(xdt, c, INNER)[:, HEAD * h:HEAD * h + HEAD], mix[:, c % 2, h, :],
                          start=True, stop=True)
            mm.matmul(bank(B_Y, 128, 256), buf(st, c, CHUNK)[0:64, :], c_of(at),
                      start=True, stop=True)
            mm.matmul(bank(B_Y + 1, 128, 256), buf(st, c, CHUNK)[64:128, :], xs_of(at)[64:128, 2, :],
                      start=True, stop=True).then_inc(S["b_done"], 1)

        def image_rows(d, q):
            v = seq[:, d, :].rearrange("p (a b) -> p a b", b=64)
            if d == 0:
                return [(v[:, 8 * q:8 * q + 8, :], slice(0, 8), slice(0, 64))]
            if d == 1:
                return [(v[:, :, 8 * q:8 * q + 8].rearrange("p w h -> p h w"), slice(0, 8), slice(0, 64))]
            if d == 2:
                return [(v[:, 8 * q:8 * q + 8:2, :], slice(0, 8, 2), slice(0, 64)),
                        (v[:, 8 * q + 1:8 * q + 8:2, ::-1], slice(1, 8, 2), slice(0, 64))]
            hi, lo = 63 - 8 * q, 63 - 8 * q - 8
            back = v[:, 1::2, hi:lo:-1] if lo >= 0 else v[:, 1::2, hi::-1]
            return [(v[:, 0::2, 8 * q:8 * q + 8].rearrange("p w h -> p h w"), slice(0, 8), slice(0, 64, 2)),
                    (back.rearrange("p w h -> p h w"), slice(0, 8), slice(1, 64, 2))]

        POST = 14

        def step(eng, b, n):
            eng.wait_ge(S["post_step"], POST * b + n)

        def pe_post(pe, b):
            mm = nc.tensor
            bar(pe, b, 15)
            for q in range(TPD):
                o = bank(q % 4).rearrange("p (h w) -> p h w", w=64)
                n = TPD * b + q
                if q >= 4:
                    pe.wait_ge(S["proj_evac"], n - 3)
                for d in range(DIRS):
                    for src, rows, cols in image_rows(d, q):
                        mm.matmul(o[:, rows, cols], pw_t[:, 128 * (d + 1):128 * (d + 2)], src,
                                  start=(d == 0), stop=False, skip_group_check=True)
                mm.matmul(bank(q % 4), pw_t[:, 0:128], local[:, 512 * q:512 * q + 512], start=False, stop=True,
                          skip_group_check=True).then_inc(S["proj_ready"], 1)
            step(pe, b, 1)
            mm.matmul(bank(4, 0, BRANCHES), ones[:, :], small[:, 0:5], start=True, stop=True)\
                .then_inc(S["post_step"], 1)
            step(pe, b, 9)
            mm.matmul(bank(5, 0, 1), const[:, C_GROUP:C_GROUP + 128], small[:, 20:21], start=True, stop=True)\
                .then_inc(S["post_step"], 1)
            step(pe, b, 12)
            mm.matmul(bank(6, 0, 1), const[:, C_GROUP:C_GROUP + 128], small[:, 24:25], start=True, stop=True)\
                .then_inc(S["post_step"], 1)
            bar(pe, b, 16)

        def pe_program(pe):
            pe_setup(pe)
            with pe.Fori(0, BATCH) as b:
                pe_prep(pe, b)
                run_tiles(pe, b, pe_body)
                pe_post(pe, b)

        def act_setup(act):
            barrier(act, 0)
            barrier(act, 1)
            barrier(act, 2)
            barrier(act, 3)
            barrier(act, 4)
            act.activation(small[:, 43:44], small[:, 41:42], ACT.Exp)
            barrier(act, 5)
            barrier(act, 6)

        def act_prep(act, b):
            bar(act, b, 0)
            bar(act, b, 1)
            img = seq[:, 0, :].rearrange("p (h w) -> p h w", w=64)
            act.activation(seq[:, 1, :].rearrange("p (w h) -> p h w", h=64), img, ACT.Copy)
            bar(act, b, 2)
            act.activation(local[:, :], local[:, :], ACT.Gelu_apprx_tanh, accum_out=sums[:, 0:1])
            bar(act, b, 3)
            P_ = S["prep_step"]
            act.activation(work1, ps[:, :], ACT.Abs, bias=dirpar[:, 1:2]).then_inc(P_, 1)
            act.activation(work2, ps[:, :], ACT.Relu, bias=dirpar[:, 1:2])
            act.wait_ge(P_, 3 * b + 1)
            act.activation(work1, work1, ACT.Exp, scale=-1.0).then_inc(P_, 1)
            act.wait_ge(P_, 3 * b + 2)
            act.activation(work1, work1, ACT.Ln, bias=1.0).then_inc(P_, 1)
            bar(act, b, 4)
            bar(act, b, 5)
            bar(act, b, 6)
            tok = ps[:, :].rearrange("p (j d r h) -> p j d r h", j=NCHUNK, d=DIRS, r=REP)
            for d in range(DIRS):
                act.activation(tab_view(wdt_tok)[:, d], tok[:, :, d, 0, :], ACT.Copy)
            bar(act, b, 7)
            bar(act, b, 8)
            bar(act, b, 9)
            bar(act, b, 10)
            for m in range(2):
                half = slice(64 * m, 64 * m + 64)
                act.activation(dec_bc[half, :].rearrange("p (k h) -> p k h", h=4),
                               ps[half, 0:1024].rearrange("p (k h) -> p k h", h=HEADS)[:, :, 4 * m:4 * m + 4], ACT.Exp)
            bar(act, b, 11)
            bar(act, b, 12)
            act.activation(wdt_tok[:, :], wdt_tok[:, :], ACT.Exp)
            bar(act, b, 13)
            bar(act, b, 14)

        def tab_view(tab):
            return tab[:, :].rearrange("p (d j h) -> p d j h", d=DIRS, j=NCHUNK)

        def act_body(act, b, t, odd):
            i = t + 1
            for c in range(CPT):
                if c == 0:
                    tanh_z(act, b, t, 0)
                if alive(t):
                    k = chunk_no(b, t, c)
                    act.wait_ge(S["tbank_ready"], k + 1)
                    earlier(act, "x_ready", b, t, c, 2)
                    earlier(act, "st_ready", b, t, c, 2)
                    earlier(act, "m_ready", b, t, c, 2)
                    act.activation(buf(xbg, c, 448), bank(B_T, 0, 448), ACT.Copy).then_inc(S["xbg_ready"], 1)
                    act.wait_ge(S["d_ready"], k + 1)
                    act.activation(decay[:, c % 2].rearrange("p h t -> p (h t)"), ps[:, 512 * B_D:512 * B_D + 1024],
                                   ACT.Exp).then_inc(S["l_ready"], 1)
                if c == 0:
                    evac_xbc(act, b, i, 1)
                if c == 1:
                    evac_xbc(act, b, i, 2)
                    exp_cs(act, b, t, 1)
                if c == 3:
                    exp_cs(act, b, i, 0)
                tq, cq = lagged(t, c, 3)
                if alive(tq):
                    k = chunk_no(b, tq, cq)
                    act.wait_ge(S["yg_ready"], k + 1)
                    if not first(tq):
                        act.wait_ge(S["ss_ready"], tile_no(b, tq))
                    sl = slice(CHUNK * cq, CHUNK * cq + CHUNK)
                    act.activation(two(sq[:, :])[:, :, sl],
                                   two(ygs[odd if c >= 3 else 1 - odd][:, :])[:, :, sl], ACT.Square)\
                        .then_inc(S["sq_ready"], 1)
                if c < XBLK and alive(i):
                    n = tile_no(b, i)
                    act.wait_ge(S["conv_done"], 3 * n + c + 1)
                    if not first(i):
                        act.wait_ge(S["silu_done"], CPT * n)
                    act.activation(tanh[:, c, :], conv[:, c, :], ACT.Tanh).then_inc(S["tanh_done"], 1)
                if c == 2:
                    if alive(t - 1):
                        n = tile_no(b, t - 1)
                        act.wait_ge(S["ss_ready"], n + 1)
                        if not first(t - 1):
                            act.wait_ge(S["r_ready"], n)
                        act.activation(var[:, :], bank(B_PZ, 0, CPT), ACT.Copy, scale=1.0 / INNER)\
                            .then_inc(S["ss_evac"], 1)
                    evac_xbc(act, b, i + 1, 0)
                    tanh_z(act, b, t, 1)
                if c == 3:
                    if alive(t - 1):
                        n = tile_no(b, t - 1)
                        act.wait_ge(S["rbc_mm"], n + 1)
                        if not first(t - 1):
                            act.wait_ge(S["o_evac"], n)
                        act.activation(rbc[:, :], bank(B_PZ), ACT.Copy).then_inc(S["rbc_ready"], 1)

        def evac_xbc(act, b, i, j):
            if not alive(i):
                return
            n = tile_no(b, i)
            act.wait_ge(S["xbc_ready"], 3 * n + j + 1)
            if not first(i):
                act.wait_ge(S["conv_done"], 3 * n + j - 2)
            act.activation(raw[:, j, 3:3 + TILE], bank(B_PX), ACT.Copy).then_inc(S["xbc_evac"], 1)

        def tanh_z(act, b, tile, pair):
            if not alive(tile):
                return
            n = tile_no(b, tile)
            act.wait_ge(S["z_ready"], 2 * n + pair + 1)
            if not (first(tile) and pair == 0):
                act.wait_ge(S["gate_done"], 2 * n + pair)
            act.activation(thz[:, :], bank(B_PZ), ACT.Tanh, scale=0.5).then_inc(S["thz_ready"], 1)

        def exp_cs(act, b, tile, pair):
            if not alive(tile):
                return
            n = tile_no(b, tile)
            act.wait_ge(S["e_ready"], 2 * n + pair + 1)
            if not first(tile):
                act.wait_ge(S["y1_done"], CPT * n - CPT + 2 * pair + 2)
            act.activation(ecs[:, TILE * pair:TILE * pair + TILE], bank(B_PZ), ACT.Exp).then_inc(S["ecs_ready"], 1)

        def act_post(act, b):
            bar(act, b, 15)
            for q in range(TPD):
                act.wait_ge(S["proj_ready"], TPD * b + q + 1)
                act.activation(work1[:, 512 * q:512 * q + 512], bank(q % 4), ACT.Copy).then_inc(S["proj_evac"], 1)
            step(act, b, 4)
            act.activation(small[:, 8:10], small[:, 8:10], ACT.Gelu_apprx_tanh).then_inc(S["post_step"], 1)
            step(act, b, 6)
            act.activation(small[:, 12:17], small[:, 12:17], ACT.Tanh, scale=0.5).then_inc(S["post_step"], 1)
            step(act, b, 14)
            for q in range(4):
                act.activation(work1[:, 1024 * q:1024 * q + 1024], work1[:, 1024 * q:1024 * q + 1024],
                               ACT.Gelu_apprx_tanh, scale=small[:, 28:29], bias=small[:, 29:30])\
                    .then_inc(S["stat_step"], 1)
            bar(act, b, 16)

        def act_program(act):
            act_setup(act)
            with act.Fori(0, BATCH) as b:
                act_prep(act, b)
                run_tiles(act, b, act_body)
                act_post(act, b)

        def dve_setup(dve):
            v = nc.vector
            v.memset(ones[:, :], 1.0)
            v.memset(small[:, 32:64], -0.5)
            v.memset(half_pow[:, :], -0.5)
            v.memset(st[:, :], 0.0)
            barrier(dve, 0)
            barrier(dve, 1)
            v.tensor_copy(pw_t[:, :].rearrange("p (k o) -> p k o", k=BRANCHES),
                          ps[:, 0:BRANCHES * 512].rearrange("p (k o) -> p k o", k=BRANCHES)[:, :, 0:128])
            v.tensor_copy(posw_t[:, :], bank(5, 0, 128))
            v.tensor_copy(nw_t[:, :], bank(6, 0, 8))
            v.tensor_scalar(taps[:, :].rearrange("p (d j k) -> p d j k", d=DIRS, j=XBLK),
                            bank(6, 16, 64).rearrange("p (j d k) -> p d j k", j=XBLK, d=DIRS), 0.5, None, ALU.mult)
            v.tensor_copy(vbc[:, :], bank(7, 0, V_COLS))
            for q in range(4):
                rows = slice(32 * q, 32 * q + 32)
                v.tensor_copy(d_col[rows, :], ps[rows, 512 * 7 + V_DP + q:512 * 7 + V_DP + 32:4])
            v.tensor_copy(wdt[:, :].rearrange("p (d r h) -> p d r h", d=DIRS, r=REP),
                          small[:, 0:32].rearrange("p (d h) -> p d h", d=DIRS).unsqueeze(2)
                          .broadcast_to([128, DIRS, REP, HEADS]))
            v.tensor_copy(ident_b[:, :], ident)
            v.tensor_copy(later[:, :], const[:, C_TRI:C_TRI + 128])
            v.tensor_copy(neg[:, :], const[:, C_NEG:C_NEG + 32])
            v.tensor_copy(sel[:, :], const[:, C_SEL:C_SEL + 32])
            v.tensor_copy(sel_e[:, :].rearrange("p (n s) -> p n s", s=HEAD),
                          const[:, C_SEL:C_SEL + 32].unsqueeze(2).broadcast_to([128, 32, HEAD]))
            barrier(dve, 2)
            v.tensor_tensor(arena2[:, 0:32], vbc[:, V_ALOG:V_ALOG + 32], const[:, C_SEL:C_SEL + 32], ALU.mult)
            v.tensor_tensor(arena2[:, 32:64], vbc[:, V_DTB:V_DTB + 32], const[:, C_SEL:C_SEL + 32], ALU.mult)
            for d in range(DIRS):
                for m in range(2):
                    w = wo_all[:, (2 * d + m) * CH:(2 * d + m + 1) * CH]
                    v.tensor_scalar(w, w, nw_t[:, 2 * d + m:2 * d + m + 1], None, ALU.mult)
            barrier(dve, 3)
            v.reduce_sum(small[:, 41:42], arena2[:, 0:32], AX_X)
            v.reduce_sum(dirpar[:, 1:2], arena2[:, 32:64], AX_X)
            v.tensor_copy(pos[:, 0:64], bank(0, 0, 64))
            v.tensor_copy(pos[:, 64:128], bank(1, 0, 64))
            barrier(dve, 4)
            barrier(dve, 5)
            v.tensor_tensor(dirpar[:, 0:1], small[:, 43:44], const[:, C_GE0:C_GE0 + 1], ALU.mult)
            barrier(dve, 6)

        def dve_prep(dve, b):
            v = nc.vector
            bar(dve, b, 0)
            img = seq[:, 0, :].rearrange("p (h w) -> p h w", w=64)
            LS = S["local_step"]
            n_local = 11
            v.tensor_tensor(img, img, pos[:, 0:64].unsqueeze(2).broadcast_to([128, 64, 64]), ALU.add).then_inc(LS, 1)
            dve.wait_ge(LS, n_local * b + 1)
            v.tensor_tensor(img, img, pos[:, 64:128].unsqueeze(1).broadcast_to([128, 64, 64]), ALU.add)\
                .then_inc(LS, 1)
            bar(dve, b, 1)
            acc = local[:, :].rearrange("p (h w) -> p h w", w=64)
            v.tensor_scalar(acc, img, lw[:, 4:5], None, ALU.mult).then_inc(LS, 1)
            n = 3
            for dh in (-1, 0, 1):
                for dw in (-1, 0, 1):
                    if dh == 0 and dw == 0:
                        continue
                    h0, h1 = max(0, -dh), 64 - max(0, dh)
                    w0, w1 = max(0, -dw), 64 - max(0, dw)
                    tap = 3 * (dh + 1) + dw + 1
                    dve.wait_ge(LS, n_local * b + n)
                    v.scalar_tensor_tensor(acc[:, h0:h1, w0:w1], img[:, h0 + dh:h1 + dh, w0 + dw:w1 + dw],
                                           lw[:, tap:tap + 1], acc[:, h0:h1, w0:w1], ALU.mult, ALU.add)\
                        .then_inc(LS, 1)
                    n += 1
            bar(dve, b, 2)
            v.memset(sums[:, 1:TPD], 0.0)
            bar(dve, b, 3)
            bar(dve, b, 4)
            SC = S["scan_step"]
            n_scan = 7
            v.tensor_tensor(work1, work1, work2, ALU.add).then_inc(SC, 1)
            dve.wait_ge(SC, n_scan * b + 1)
            v.tensor_scalar(work2, work1, dirpar[:, 0:1], None, ALU.mult).then_inc(SC, 1)
            dve.wait_ge(SC, n_scan * b + 2)
            for j in range(NCHUNK):
                w = work2[:, 128 * j:128 * j + 128]
                v.tensor_tensor_scan(w, ones[:, :], w, 0.0, ALU.mult, ALU.add)
            bar(dve, b, 5)
            v.tensor_copy(csp[:, :], work2).then_inc(SC, 1)
            bar(dve, b, 6)
            v.scalar_tensor_tensor(work2, csp[:, :], const[:, C_GE1:C_GE1 + 1], work2, ALU.mult, ALU.add)\
                .then_inc(SC, 1)
            dve.wait_ge(SC, n_scan * b + 4)
            v.tensor_copy(csp[:, :], work2).then_inc(SC, 1)
            dve.wait_ge(SC, n_scan * b + 5)
            v.scalar_tensor_tensor(work2, csp[:, :], const[:, C_GE2:C_GE2 + 1], work2, ALU.mult, ALU.add)\
                .then_inc(SC, 1)
            dve.wait_ge(SC, n_scan * b + 6)
            v.tensor_copy(csp[:, :], work2).then_inc(SC, 1)
            bar(dve, b, 7)
            bar(dve, b, 8)
            tok = ps[:, :].rearrange("p (j d r h) -> p j d r h", j=NCHUNK, d=DIRS, r=REP)
            for d in range(DIRS):
                v.tensor_copy(tab_view(dt_tok)[:, d], tok[:, :, d, 0, :])
            bar(dve, b, 9)
            bar(dve, b, 10)
            bar(dve, b, 11)
            v.tensor_tensor(wdt_tok[:, :], ps[:, 0:1024], wdt_tok[:, :], ALU.subtract)
            bar(dve, b, 12)
            bar(dve, b, 13)
            v.tensor_tensor(wdt_tok[:, :], wdt_tok[:, :], dt_tok[:, :], ALU.mult).then_inc(S["wdt_step"], 1)
            dve.wait_ge(S["wdt_step"], b + 1)
            v.memset(tab_view(wdt_tok)[:, :, NCHUNK - 1, :], 0.0)
            v.memset(dec_bc[:, :].rearrange("p (d j h) -> p d j h", d=DIRS, h=4)[:, :, NCHUNK - 1, :], 0.0)
            v.memset(raw[:, :, 0:3], 0.0)
            bar(dve, b, 14)

        def dve_body(dve, b, t, odd):
            v = nc.vector
            i = t + 1
            for c in range(CPT):
                if c == 0:
                    gate_z(dve, b, t, 0)
                    scale_out(dve, b, t - 2)
                if c == 3:
                    gate_z(dve, b, t, 1)
                if c < XBLK and alive(i):
                    convolve(dve, b, i, c)
                if c == 3:
                    for cc in range(2):
                        silu(dve, b, i, cc, odd)
                tb, cb = lagged(t, c, 1)
                if alive(tb):
                    k = chunk_no(b, tb, cb)
                    dve.wait_ge(S["st_ready"], k + 1)
                    dve.wait_ge(S["sdec_ready"], k + 1)
                    earlier(dve, "b_done", b, tb, cb, 1)
                    v.tensor_tensor(buf(st, cb + 1, CHUNK), bank(B_S, 0, CHUNK), st_dec[:, :], ALU.add)\
                        .then_inc(S["s_upd"], 1)
                if alive(t):
                    k = chunk_no(b, t, c)
                    dve.wait_ge(S["l_ready"], k + 1)
                    earlier(dve, "b_done", b, t, c, 2)
                    v.tensor_tensor(mix[:, c % 2], decay[:, c % 2],
                                    buf(xbg, c, 448)[:, 320:448].unsqueeze(1).broadcast_to([128, HEADS, CHUNK]),
                                    ALU.mult).then_inc(S["m_ready"], 1)
                if alive(tb):
                    k = chunk_no(b, tb, cb)
                    earlier(dve, "yg_ready", b, tb, cb, 2)
                    dve.wait_ge(S["ecs_ready"], 2 * tile_no(b, tb) + cb // 2 + 1)
                    dve.wait_ge(S["b_done"], k + 1)
                    earlier(dve, "ysum_done", b, tb, cb, 1)
                    v.tensor_tensor(two(y1[:, :]), y_banks[:, :, 128:256], pair_of(ecs, cb), ALU.mult)\
                        .then_inc(S["y1_done"], 1)
                    dve.wait_ge(S["y1_done"], k + 1)
                    v.tensor_tensor(two(buf(y2, cb, INNER)), y_banks[:, :, 0:128], two(y1[:, :]), ALU.add)\
                        .then_inc(S["ysum_done"], 1)
                if c == 3:
                    silu(dve, b, i, 2, odd)
                    silu(dve, b, i, 3, odd)

        def scale_out(dve, b, tile):
            if not alive(tile):
                return
            n = tile_no(b, tile)
            dve.wait_ge(S["out_ready"], n + 1)
            dve.wait_ge(S["rbc_ready"], n + 1)
            nc.vector.scalar_tensor_tensor(useq[:, bass.ds(tile * TILE, TILE)], bank(B_PX), 1.0, rbc[:, :],
                                           ALU.mult, ALU.mult, accum_out=sums[:, bass.ds(TPD + tile, 1)])\
                .then_inc(S["o_evac"], 1)

        def convolve(dve, b, i, j):
            v = nc.vector
            n = XBLK * tile_no(b, i) + j
            dve.wait_ge(S["xbc_evac"], n + 1)
            if not first(i):
                dve.wait_ge(S["conv_done"], n - 2)
                if j == 0:
                    dve.wait_ge(S["silu_done"], CPT * tile_no(b, i))
            for k in range(TAPS):
                w = taps[:, bass.ds(i // TPD * XBLK * TAPS + j * TAPS + k, 1)]
                if k == 0:
                    v.tensor_scalar(conv[:, j, :], raw[:, j, 0:TILE], w, None, ALU.mult).then_inc(S["tap_done"], 1)
                else:
                    dve.wait_ge(S["tap_done"], TAPS * n + k)
                    v.scalar_tensor_tensor(conv[:, j, :], raw[:, j, k:k + TILE], w, conv[:, j, :],
                                           ALU.mult, ALU.add).then_inc(S["tap_done"], 1)
            v.tensor_scalar(raw[:, j, 0:3], raw[:, j, TILE:TILE + 3], const[:, bass.ds(C_FLAG + i + 1, 1)], None,
                            ALU.mult).then_inc(S["conv_done"], 1)

        def gate_z(dve, b, tile, pair):
            if not alive(tile):
                return
            n = tile_no(b, tile)
            dve.wait_ge(S["thz_ready"], 2 * n + pair + 1)
            if not first(tile):
                dve.wait_ge(S["yg_ready"], CPT * n - CPT + 2 * pair + 2)
            nc.vector.scalar_tensor_tensor(gate[:, TILE * pair:TILE * pair + TILE], thz[:, :], 1.0, bank(B_PZ),
                                           ALU.add, ALU.mult).then_inc(S["gate_done"], 1)

        def silu(dve, b, i, c, odd):
            if not alive(i):
                return
            v = nc.vector
            dve.wait_ge(S["tanh_done"], 3 * tile_no(b, i) + 3)
            if not isinstance(i, int) or i >= 2:
                k = chunk_no(b, i, c) - 2 * CPT
                dve.wait_ge(S["tbank_ready"], k + 1)
                dve.wait_ge(S["x_ready"], k + 1)
                dve.wait_ge(S["b_done"], k + 1)
            cols = slice(128 * c, 128 * c + 128)
            v.scalar_tensor_tensor(xs_of(slot(odd, c, -CPT)), tanh[:, :, cols], 1.0, conv[:, :, cols], ALU.add, ALU.mult)
            v.scalar_tensor_tensor(c_of(slot(odd, c, -CPT)), tanh[64:128, 2, cols], 1.0, conv[64:128, 2, cols],
                                   ALU.add, ALU.mult).then_inc(S["silu_done"], 1)

        def order_parts(d):
            im = lambda x: x.rearrange("p (h w) -> p h w", w=64)
            s = seq[:, d, :].rearrange("p (a b) -> p a b", b=64)
            if d == 0:
                return [(lambda x: im(x), s)]
            if d == 1:
                return [(lambda x: im(x), s.rearrange("p w h -> p h w"))]
            if d == 2:
                return [(lambda x: im(x)[:, 0::2, :], s[:, 0::2, :]),
                        (lambda x: im(x)[:, 1::2, :], s[:, 1::2, ::-1])]
            return [(lambda x: im(x)[:, :, 0::2].rearrange("p h w -> p w h"), s[:, 0::2, :]),
                    (lambda x: im(x)[:, :, 1::2].rearrange("p h w -> p w h"), s[:, 1::2, ::-1])]

        def dve_post(dve, b):
            v = nc.vector
            bar(dve, b, 15)
            P_ = S["post_step"]
            v.reduce_sum(small[:, 0:5], sums[:, :].rearrange("p (k t) -> p k t", k=BRANCHES), AX_X).then_inc(P_, 1)
            step(dve, b, 2)
            w1 = vbc[:, V_W1:V_W1 + 10].rearrange("p (i j) -> p j i", j=2)
            desc = bank(4, 0, BRANCHES).unsqueeze(1).broadcast_to([128, 2, BRANCHES])
            v.scalar_tensor_tensor(small[:, 44:54].rearrange("p (j i) -> p j i", j=2), desc, 1.0 / (CH * PIX), w1,
                                   ALU.mult, ALU.mult).then_inc(P_, 1)
            step(dve, b, 3)
            SS = S["fuse_step"]
            n_fuse = 8
            v.reduce_sum(small[:, 6:8], small[:, 44:54].rearrange("p (j i) -> p j i", j=2), AX_X).then_inc(SS, 1)
            dve.wait_ge(SS, n_fuse * b + 1)
            v.tensor_tensor(small[:, 8:10], small[:, 6:8], vbc[:, V_B1:V_B1 + 2], ALU.add).then_inc(P_, 1)
            step(dve, b, 5)
            w2 = vbc[:, V_W2:V_W2 + 10].rearrange("p (j i) -> p i j", j=2)
            v.tensor_tensor(small[:, 44:54].rearrange("p (i j) -> p i j", j=2),
                            small[:, 8:10].unsqueeze(1).broadcast_to([128, BRANCHES, 2]), w2, ALU.mult).then_inc(SS, 1)
            dve.wait_ge(SS, n_fuse * b + 2)
            v.reduce_sum(small[:, 54:59], small[:, 44:54].rearrange("p (i j) -> p i j", j=2), AX_X).then_inc(SS, 1)
            dve.wait_ge(SS, n_fuse * b + 3)
            v.tensor_tensor(small[:, 12:17], small[:, 54:59], vbc[:, V_B2:V_B2 + 5], ALU.add).then_inc(P_, 1)
            step(dve, b, 7)
            v.tensor_scalar(small[:, 12:17], small[:, 12:17], 0.5, 0.5, ALU.mult, ALU.add).then_inc(P_, 1)
            stats = gate[:, 0:6 * TPD]
            for q in range(TPD):
                dve.wait_ge(S["proj_evac"], TPD * b + q + 1)
                last = v.bn_stats(stats[:, 6 * q:6 * q + 6], work1[:, 512 * q:512 * q + 512])
            last.then_inc(SS, 1)
            dve.wait_ge(SS, n_fuse * b + 4)
            step(dve, b, 8)
            settle(dve)
            v.bn_aggr(small[:, 20:22], stats).then_inc(P_, 1)
            step(dve, b, 10)
            v.tensor_copy(small[:, 22:23], bank(5, 0, 1)).then_inc(SS, 1)
            dve.wait_ge(SS, n_fuse * b + 5)
            v.tensor_tensor(small[:, 23:24], small[:, 20:21], small[:, 22:23], ALU.subtract).then_inc(P_, 1)
            step(dve, b, 11)
            v.scalar_tensor_tensor(small[:, 24:25], small[:, 23:24], small[:, 23:24], small[:, 21:22],
                                   ALU.mult, ALU.add).then_inc(P_, 1)
            step(dve, b, 13)
            v.tensor_scalar(small[:, 25:26], bank(6, 0, 1), EPS, None, ALU.add).then_inc(SS, 1)
            dve.wait_ge(S["var_done"], (TILES + 1) * b + TILES + 1)
            v.tensor_tensor(small[:, 28:29], small[:, 26:27], gnp[:, 0:1], ALU.mult).then_inc(SS, 1)
            dve.wait_ge(SS, n_fuse * b + 7)
            v.tensor_tensor(small[:, 27:28], small[:, 28:29], small[:, 22:23], ALU.mult).then_inc(SS, 1)
            dve.wait_ge(SS, n_fuse * b + 8)
            v.tensor_tensor(small[:, 29:30], gnp[:, 1:2], small[:, 27:28], ALU.subtract).then_inc(P_, 1)
            dve.wait_ge(S["x_loaded"], 32 * b + 32)
            FS = S["tap_done_post"]
            n = 0
            v.scalar_tensor_tensor(work2, local[:, :], small[:, 12:13], work2, ALU.mult, ALU.add).then_inc(FS, 1)
            for d in range(DIRS):
                n += 1
                dve.wait_ge(FS, 5 * b + n)
                for pick, src in order_parts(d):
                    last = v.scalar_tensor_tensor(pick(work2), src, small[:, 13 + d:14 + d], pick(work2),
                                                  ALU.mult, ALU.add)
                last.then_inc(FS, 1)
            dve.wait_ge(FS, 5 * b + 5)
            for q in range(4):
                dve.wait_ge(S["stat_step"], 4 * b + q + 1)
                w = slice(1024 * q, 1024 * q + 1024)
                v.tensor_tensor(work2[:, w], work2[:, w], work1[:, w], ALU.add).then_inc(S["part_ready"], 1)
            bar(dve, b, 16)

        S["tap_done_post"] = sem("branch_added")

        def dve_program(dve):
            dve_setup(dve)
            with dve.Fori(0, BATCH) as b:
                dve_prep(dve, b)
                run_tiles(dve, b, dve_body)
                dve_post(dve, b)

        def pool_setup(pool):
            for n in range(SETUP_BARS):
                barrier(pool, n)

        def pool_prep(pool, b):
            g = nc.gpsimd
            bar(pool, b, 0)
            bar(pool, b, 1)
            img = seq[:, 0, :].rearrange("p (h w) -> p h w", w=64)
            for d in (2, 3):
                for pick, dst in order_parts(d):
                    g.tensor_copy(dst, pick(seq[:, 0, :]))
            for n in range(2, 15):
                bar(pool, b, n)

        def pool_body(pool, b, t, odd):
            g = nc.gpsimd
            for c in range(CPT):
                ty, cy = lagged(t, c, 2)
                if alive(ty):
                    k = chunk_no(b, ty, cy)
                    pool.wait_ge(S["x_ready"], k + 1)
                    pool.wait_ge(S["ysum_done"], k + 1)
                    y_, xd_ = buf(y2, cy, INNER), buf(xd, cy, INNER)
                    g.tensor_tensor(y_, y_, xd_, ALU.add).then_inc(S["y3_done"], 1)
                    pool.wait_ge(S["gate_done"], 2 * tile_no(b, ty) + cy // 2 + 1)
                    if not first(ty):
                        pool.wait_ge(S["sq_ready"], chunk_no(b, ty, cy) - 3)
                    if not isinstance(ty, int) or ty >= 2:
                        pool.wait_ge(S["out_ready"], tile_no(b, ty) - 1)
                    pool.wait_ge(S["y3_done"], k + 1)
                    g.tensor_tensor(two(ygs[odd if c >= 2 else 1 - odd][:, :])[:, :, CHUNK * cy:CHUNK * cy + CHUNK], two(y_),
                                    pair_of(gate, cy), ALU.mult).then_inc(S["yg_ready"], 1)
                if c == 3 and alive(t - 1):
                    n = tile_no(b, t - 1)
                    pool.wait_ge(S["ss_evac"], n + 1)
                    settle(pool)
                    g.tensor_scalar(var[:, :], var[:, :], 4 * EPS, None, ALU.add).then_inc(S["var_done"], 1)
                    if not first(t - 1):
                        pool.wait_ge(S["rbc_mm"], n)
                    pool.wait_ge(S["var_done"], n + b + 1)
                    g.tensor_tensor(rms[:, :], var[:, :], half_pow[:, :], ALU.pow).then_inc(S["r_ready"], 1)
                if alive(t):
                    k = chunk_no(b, t, c)
                    earlier(pool, "b_done", b, t, c, 2)
                    pool.wait_ge(S["xbg_ready"], k + 1)
                    settle(pool)
                    x_ = by_head(buf(xbg, c, 448)[:, 0:256])
                    g.tensor_tensor(by_head(buf(xw, c, INNER)), x_, table(wdt_tok, t, c), ALU.mult)
                    g.tensor_tensor(by_head(buf(xdt, c, INNER)), x_, table(dt_tok, t, c), ALU.mult)
                    dp = d_col[:, bass.ds(t // TPD * 2, 2)].unsqueeze(2).broadcast_to([128, 2, CHUNK])
                    earlier(pool, "yg_ready", b, t, c, 2)
                    settle(pool)
                    g.tensor_tensor(two(buf(xd, c, INNER)), xs_of(slot(odd, c))[:, 0:2, :], dp, ALU.mult)\
                        .then_inc(S["x_ready"], 1)
                    earlier(pool, "s_upd", b, t, c, 1)
                    settle(pool)
                    g.tensor_tensor(st_dec[:, :].rearrange("p (h d) -> p h d", h=4),
                                    buf(st, c, CHUNK).rearrange("p (h d) -> p h d", h=4), table(dec_bc, t, c, 4),
                                    ALU.mult).then_inc(S["sdec_ready"], 1)

        def pool_post(pool, b):
            bar(pool, b, 15)
            pool.wait_ge(S["fuse_step"], 8 * b + 6)
            nc.gpsimd.tensor_tensor(small[:, 26:27], small[:, 25:26], small[:, 60:61], ALU.pow)\
                .then_inc(S["var_done"], 1)
            bar(pool, b, 16)

        def pool_program(pool):
            pool_setup(pool)
            with pool.Fori(0, BATCH) as b:
                pool_prep(pool, b)
                run_tiles(pool, b, pool_body)
                pool_post(pool, b)

        block = ctx.enter_context(nc.Block())

        @block.sync
        def _(sp):
            sp_program(sp)

        @block.tensor
        def _(pe):
            pe_program(pe)

        @block.scalar
        def _(act):
            act_program(act)

        @block.vector
        def _(dve):
            dve_program(dve)

        @block.gpsimd
        def _(pool):
            pool_program(pool)


_INS = ["x", "L0_conv_pos_proj_w", "L0_conv_local_w", "L0_conv_W_in", "L0_conv_conv_w", "L0_conv_A_log",
        "L0_conv_dt_bias", "L0_conv_Dp", "L0_conv_norm_w", "L0_conv_W_out", "L0_conv_se_w1", "L0_conv_se_b1",
        "L0_conv_se_w2", "L0_conv_se_b2", "L0_conv_proj_w", "L0_conv_gn_gamma", "L0_conv_gn_beta"]


def kernel(**inputs):
    import concourse.bacc as _bacc
    from concourse.bass_utils import run_bass_kernel_spmd as _run

    nc = _bacc.Bacc("TRN2", target_bir_lowering=False, num_devices=1)
    arrays, aps = {}, {}
    for name in _INS:
        arr = np.ascontiguousarray(inputs[name])
        arrays[f"in_{name}_dram"] = arr
        aps[name.replace("L0_conv_", "")] = nc.dram_tensor(
            f"in_{name}_dram", arr.shape, mybir.dt.from_np(arr.dtype), kind="ExternalInput").ap()
    arrays["shape_const_dram"] = shape_constants()
    aps["shape_const"] = nc.dram_tensor("shape_const_dram", (128, C_COLS), F32, kind="ExternalInput").ap()
    out = nc.dram_tensor("out_0_dram", (BATCH, CH, HEIGHT, WIDTH), F32, kind="ExternalOutput").ap()
    build(nc, aps, out)
    r = _run(nc, [arrays], core_ids=[0])
    return r.results[0]["out_0_dram"]
```

```python
from contextlib import ExitStack

import numpy as np
import concourse.bass as bass
from concourse import mybir

F32 = mybir.dt.float32
BF16 = mybir.dt.bfloat16
ALU = mybir.AluOpType
ACT = mybir.ActivationFunctionType
AX_X = mybir.AxisListType.X

BATCH, CH, HEIGHT, WIDTH = 8, 128, 64, 64
PIX = HEIGHT * WIDTH
DIRS = 4
STATE = 64
HEADS, HEAD = 8, 32
INNER = HEADS * HEAD
CONV = INNER + 2 * STATE
XBLK = CONV // 128
TAPS = 4
CHUNK = 128
TILE = 512
CPT = TILE // CHUNK
TPD = PIX // TILE
TILES = DIRS * TPD
NCHUNK = PIX // CHUNK
BRANCHES = 5
GROUP = CH // 8
REP = 4
SPLIT = 3
EPS = 1e-5

C_IDENT, C_TRI, C_LAST, C_GROUP, C_POS = 0, 128, 256, 384, 512
C_SEL, C_NEG, C_FLAG, C_GE1, C_GE2, C_GE0 = 576, 608, 640, 680, 681, 682
C_COLS = 683
V_ALOG, V_DTB, V_DP, V_W1, V_B1, V_W2, V_B2 = 0, 32, 64, 96, 106, 108, 118
V_COLS = 123


def shape_constants():
    t = np.zeros((128, C_COLS), np.float32)
    i = np.arange(128)
    t[:, C_IDENT:C_IDENT + 128] = np.eye(128)
    t[:, C_TRI:C_TRI + 128] = -1e30 * (i[None, :] < i[:, None])
    t[127, C_LAST:C_LAST + 128] = 1.0
    t[:, C_GROUP:C_GROUP + 128] = (i[:, None] // GROUP == i[None, :] // GROUP) / GROUP
    half = CH // 2
    freq = 10000.0 ** (np.arange(0, half, 2, dtype=np.float32) / half)
    ph = np.arange(HEIGHT, dtype=np.float32)[:, None] / freq
    emb = np.stack([np.sin(ph), np.cos(ph)], 2).reshape(HEIGHT, -1).T
    t[0:64, C_POS:C_POS + 64] = emb
    t[64:128, C_POS:C_POS + 64] = emb
    row_dir, row_rep, row_head = i // 32, i // 8 % 4, i % 8
    for d in range(DIRS):
        for h in range(HEADS):
            own = (row_dir == d) & (row_head == h) & (row_rep < SPLIT)
            t[:, C_SEL + 8 * d + h] = own
            t[:, C_NEG + 8 * d + h] = -1.0 * own
    t[:, C_FLAG:C_FLAG + 40] = np.arange(40) % TPD != 0
    t[:, C_GE0] = -1.0 * (row_rep < SPLIT)
    t[:, C_GE1] = -1.0 * (row_rep >= 1)
    t[:, C_GE2] = -1.0 * (row_rep >= 2)
    return t


def build(nc, a, out):
    ctx = ExitStack()
    with ctx:
        def sb(name, shape, dt=F32):
            return ctx.enter_context(nc.sbuf_tensor(name, shape, dt))

        def sem(name):
            return ctx.enter_context(nc.semaphore(name))

        useq = sb("useq", [128, DIRS * PIX])
        local = sb("local", [128, PIX])
        arena1 = sb("arena1", [128, PIX])
        arena2 = sb("arena2", [128, 3 * (3 + TILE) + 6 * TILE])
        csp = sb("csp", [128, PIX], BF16)
        sel = sb("sel", [128, DIRS * HEADS], BF16)
        ident_b = sb("ident_b", [128, 128], BF16)
        later = sb("later", [128, 128], BF16)
        neg = sb("neg", [128, DIRS * HEADS], BF16)
        const = sb("const", [128, C_COLS])
        vbc = sb("vbc", [128, V_COLS])
        ones = sb("ones", [128, 128])
        dt_tok = sb("dt_tok", [128, DIRS * NCHUNK * HEADS])
        wdt_tok = sb("wdt_tok", [128, DIRS * NCHUNK * HEADS])
        dec_bc = sb("dec_bc", [128, DIRS * NCHUNK * 4])
        wz = sb("wz", [128, INNER])
        sel_e = sb("sel_e", [128, DIRS * INNER], BF16)
        wo_all = sb("wo_all", [128, DIRS * 2 * CH])
        wdt = sb("wdt", [128, DIRS * 32])
        wx = sb("wx", [128, 2 * CONV])
        wo = sb("wo", [128, 2 * CH])
        taps = sb("taps", [128, DIRS * XBLK * TAPS])
        lw = sb("lw", [128, 9])
        pw_t = sb("pw_t", [128, BRANCHES * CH])
        posw_t = sb("posw_t", [128, CH])
        pos = sb("pos", [128, 2 * 64])
        gnp = sb("gnp", [128, 2])
        nw_t = sb("nw_t", [128, 8])
        d_col = sb("d_col", [128, DIRS * 2])
        dirpar = sb("dirpar", [128, 2])
        sums = sb("sums", [128, BRANCHES * TPD])
        small = sb("small", [128, 64])
        xs = sb("xs", [128, 2 * CPT * CONV])
        c_low = sb("c_low", [64, 2 * CPT * CHUNK])
        xbg = sb("xbg", [128, 2 * 448])
        xdt = sb("xdt", [128, 2 * INNER])
        xw = sb("xw", [128, 2 * INNER])
        xd = sb("xd", [128, 2 * INNER])
        thz = sb("thz", [128, TILE])
        gate = sb("gate", [128, 2 * TILE])
        ecs = sb("ecs", [128, 2 * TILE])
        y1 = sb("y1", [128, INNER])
        y2 = sb("y2", [128, 2 * INNER])
        ygs = [sb(f"yg{n}", [128, 2 * TILE]) for n in range(2)]
        sq = sb("sq", [128, 2 * INNER])
        ssum = sb("ssum", [128, TILE])
        var = sb("var", [128, CPT])
        rms = sb("rms", [128, CPT])
        half_pow = sb("half_pow", [128, CPT])
        rbc = sb("rbc", [128, TILE])
        st = sb("st", [128, 2 * CHUNK])
        st_dec = sb("st_dec", [128, CHUNK])
        ps = ctx.enter_context(nc.psum_tensor("ps", [128, 8 * 512], F32))

        def bank(n, lo=0, hi=512):
            return ps[:, 512 * n + lo:512 * n + hi]

        B_PX, B_T, B_D, B_Y, B_PZ, B_S = 0, 1, 2, 4, 6, 7

        ident = const[:, C_IDENT:C_IDENT + 128]
        decay = arena1[:, 0:2048].rearrange("p (b h t) -> p b h t", b=2, h=HEADS)
        mix = arena1[:, 2048:4096].rearrange("p (b h t) -> p b h t", b=2, h=HEADS)
        RAW = 3 + TILE
        raw = arena2[:, 0:3 * RAW].rearrange("p (j t) -> p j t", j=XBLK)
        conv = arena2[:, 3 * RAW:3 * RAW + 3 * TILE].rearrange("p (j t) -> p j t", j=XBLK)
        tanh = arena2[:, 3 * RAW + 3 * TILE:3 * RAW + 6 * TILE].rearrange("p (j t) -> p j t", j=XBLK)
        y_banks = ps[:, 512 * B_Y:512 * B_Y + 1024].rearrange("p (m t) -> p m t", m=2)
        seq = useq[:, :].rearrange("p (d n) -> p d n", d=DIRS)
        work1, work2 = arena1[:, :], arena2[:, 0:PIX]
        vrow = arena2[0:1, 128:128 + V_COLS]

        S = {n: sem(n) for n in (
            "phase", "loaded", "x_loaded", "prep_step", "local_step", "scan_step", "post_step",
            "proj_ready", "proj_evac", "fuse_step", "stored", "part_ready", "wx_loaded",
            "wz_loaded", "wo_loaded", "xbc_ready", "z_ready", "e_ready", "xbc_evac", "thz_ready",
            "gate_done", "ecs_ready", "first_tap", "tap_done", "conv_done", "tanh_done",
            "silu_done", "tbank_ready", "d_ready", "xbg_ready", "l_ready", "x_ready", "m_ready",
            "st_ready", "sdec_ready", "s_upd", "b_done", "y1_done", "ysum_done", "y3_done",
            "yg_ready", "sq_ready", "sqs_ready", "ss_ready", "ss_evac", "var_done", "r_ready",
            "rbc_mm", "rbc_ready", "out_ready", "o_evac", "stat_step", "dt_turned", "branch_added",
            "wdt_step", "settled")}

        SETUP_BARS, BATCH_BARS = 7, 15

        def settle(eng):
            eng.sem_inc(S["settled"], 1)

        def barrier(eng, count):
            eng.drain().then_inc(S["phase"], 1)
            eng.wait_ge(S["phase"], 5 * (count + 1))
            settle(eng)

        def bar(eng, b, n):
            barrier(eng, SETUP_BARS + b * BATCH_BARS + n)

        def alive(t):
            return not isinstance(t, int) or 0 <= t < TILES

        def first(t):
            return isinstance(t, int) and t == 0

        def lagged(t, c, lag):
            return (t, c - lag) if c >= lag else (t - 1, c - lag + CPT)

        def tile_no(b, t):
            return b * TILES + t

        def chunk_no(b, t, c):
            return (b * TILES + t) * CPT + c

        def earlier(eng, name, b, t, c, lag):
            if not (first(t) and c < lag):
                eng.wait_ge(S[name], chunk_no(b, t, c) - lag + 1)

        def heads(ap, n=HEAD):
            p, h = ap.shape
            return ap.unsqueeze(2).broadcast_to([p, h, n])

        def by_head(ap):
            return ap.rearrange("p (h d) -> p h d", h=HEADS)

        def table(tab, t, c, n=HEADS):
            ap = tab[:, bass.ds((t * CPT + c) * n, n)]
            return heads(ap)

        P_USES = {B_PX: (("out", 0, -3), ("xbc", 0, 1), ("xbc", 1, 1), ("xbc", 2, 1)),
                  B_PZ: (("z", 0, -1), ("e", 1, -1), ("z", 1, -1), ("e", 0, 0))}
        READ_OUT = {"xbc": ("xbc_evac", XBLK), "out": ("o_evac", 1),
                    "z": ("gate_done", 2), "e": ("ecs_ready", 2)}

        def p_wait(pe, b, i, kind, part=0):
            uses = [u for us in P_USES.values() if (kind, part) in [x[:2] for x in us] for u in us]
            at = [u[:2] for u in uses].index((kind, part))
            for back in range(1, 4 * len(uses)):
                k, body = (at - back) % len(uses), i + (at - back) // len(uses)
                name, part_, lag = uses[k]
                if alive(body + lag):
                    evac, per = READ_OUT[name]
                    pe.wait_ge(S[evac], per * tile_no(b, body + lag) + part_ + 1)
                    return

        RING = 2 * CPT

        def slot(odd, c, lag=0):
            return (CPT * odd + c - lag) % RING

        def xs_of(s):
            return xs[:, s * CONV:s * CONV + CONV].rearrange("p (j t) -> p j t", j=XBLK)

        def c_of(s):
            return c_low[:, s * CHUNK:s * CHUNK + CHUNK]

        def pair_of(ap, c):
            return ap[:, TILE * (c // 2):TILE * (c // 2) + TILE].rearrange("p (m t) -> p m t", m=2)[
                :, :, CHUNK * (c % 2):CHUNK * (c % 2) + CHUNK]

        def two(ap):
            return ap.rearrange("p (m t) -> p m t", m=2)

        def buf(t_, c, w):
            return t_[:, (c % 2) * w:(c % 2) * w + w]

        def run_tiles(eng, b, body):
            for t in range(-2, 4):
                body(eng, b, t, t % 2)
            with eng.Fori(2, TILES // 2 - 1) as u:
                body(eng, b, u * 2, 0)
                body(eng, b, u * 2 + 1, 1)
            for t in range(TILES - 2, TILES + 2):
                body(eng, b, t, t % 2)

        def sp_setup(sp):
            L = S["loaded"]
            sp.dma_start(const[:, :], a["shape_const"]).then_inc(L, 16)
            for name, at, n in (("A_log", V_ALOG, 32), ("dt_bias", V_DTB, 32), ("Dp", V_DP, 32)):
                sp.dma_start(vrow[0:1, at:at + n], a[name].rearrange("(o d) h -> o (d h)", o=1)).then_inc(L, 16)
            for name, at, n in (("se_w1", V_W1, 10), ("se_w2", V_W2, 10)):
                sp.dma_start(vrow[0:1, at:at + n], a[name].rearrange("(o d) h -> o (d h)", o=1)).then_inc(L, 16)
            for name, at, n in (("se_b1", V_B1, 2), ("se_b2", V_B2, 5)):
                sp.dma_start(vrow[0:1, at:at + n], a[name].rearrange("(o d) -> o d", o=1)).then_inc(L, 16)
            w_in = a["W_in"].rearrange("d c n -> c d n")
            sp.dma_start(small[:, 0:32].rearrange("p (d n) -> p d n", d=DIRS),
                         w_in[:, :, INNER + CONV:INNER + CONV + HEADS]).then_inc(L, 16)
            sp.dma_start(wo_all[:, :].rearrange("p (d m o) -> p d m o", d=DIRS, m=2),
                         a["W_out"].rearrange("d (m k) o -> k d m o", m=2)).then_inc(L, 16)
            sp.dma_start(lw[:, :], a["local_w"].rearrange("c u i j -> c (u i j)")).then_inc(L, 16)
            sp.dma_start(gnp[:, 0:1], a["gn_gamma"].rearrange("(c o) -> c o", o=1)).then_inc(L, 16)
            sp.dma_start(gnp[:, 1:2], a["gn_beta"].rearrange("(c o) -> c o", o=1)).then_inc(L, 16)
            sp.dma_start(arena1[:, 0:640], a["proj_w"]).then_inc(L, 16)
            sp.dma_start(arena1[:, 640:768], a["pos_proj_w"]).then_inc(L, 16)
            sp.dma_start(arena1[0:8, 768:896], a["norm_w"].rearrange("d (m k) -> (d m) k", m=2)).then_inc(L, 16)
            sp.dma_start(arena1[0:16, 1024:1024 + CONV], a["conv_w"].rearrange("d k c -> (d k) c")).then_inc(L, 16)
            sp.wait_ge(L, 16 * 17)
            for n in range(SETUP_BARS):
                barrier(sp, n)

        def sp_body(sp, b, t, odd):
            i = t + 1
            if alive(t - 1):
                if not first(t - 1):
                    sp.wait_ge(S["out_ready"], tile_no(b, t - 1))
                    settle(sp)
                sp.dma_start(wo[:, :], wo_all[:, bass.ds((t - 1) // TPD * 2 * CH, 2 * CH)]).then_inc(S["wo_loaded"], 16)
            if alive(i + 1):
                if not (isinstance(i, int) and i <= 0):
                    sp.wait_ge(S["xbc_ready"], XBLK * tile_no(b, i))
                    settle(sp)
                if not first(i + 1):
                    sp.wait_ge(S["wx_loaded"], 16 * tile_no(b, i + 1))
                    settle(sp)
                load_w(sp, i + 1, wx[:, (1 - odd) * CONV:(2 - odd) * CONV], INNER, INNER + CONV, "wx_loaded")
            if alive(i):
                if not first(i):
                    sp.wait_ge(S["z_ready"], 2 * tile_no(b, i))
                    settle(sp)
                load_w(sp, i, wz[:, :], 0, INNER, "wz_loaded")

        def load_w(sp, i, dst, lo, hi, name):
            d = i // TPD
            w = a["W_in"][d, :, lo:hi] if isinstance(d, int) else \
                a["W_in"][bass.ds(d, 1), :, lo:hi].rearrange("d c n -> c (d n)")
            sp.dma_start(dst, w).then_inc(S[name], 16)

        def sp_program(sp):
            sp_setup(sp)
            def image(b):
                return a["x"][bass.ds(b, 1)].rearrange("b c h w -> c (b h w)")

            sp.dma_start(seq[:, 0, :], a["x"][0].rearrange("c h w -> c (h w)")).then_inc(S["x_loaded"], 16)
            with sp.Fori(0, BATCH) as b:
                sp.wait_ge(S["x_loaded"], 32 * b + 16)
                settle(sp)
                for n in range(13):
                    bar(sp, b, n)
                run_tiles(sp, b, sp_body)
                bar(sp, b, 13)
                sp.dma_start(work2, image(b)).then_inc(S["x_loaded"], 16)
                sp.wait_ge(S["x_loaded"], 32 * b + 32)
                sp.wait_ge(S["branch_added"], 5 * b + 5)
                sp.wait_ge(S["proj_ready"], TPD * b + TPD)
                settle(sp)
                sp.dma_start(seq[:, 0, :], image((b + 1) % BATCH)).then_inc(S["x_loaded"], 16)
                out_img = out[bass.ds(b, 1)].rearrange("b c h w -> c (b h w)")
                for q in range(4):
                    sp.wait_ge(S["part_ready"], 4 * b + q + 1)
                    sp.dma_start(out_img[:, q * 1024:(q + 1) * 1024], work2[:, q * 1024:(q + 1) * 1024])\
                        .then_inc(S["stored"], 16)
                sp.wait_ge(S["stored"], 64 * b + 64)
                settle(sp)
                bar(sp, b, 14)
            sp.wait_ge(S["x_loaded"], 32 * BATCH + 16)

        def pe_setup(pe):
            barrier(pe, 0)
            mm = nc.tensor
            for k in range(BRANCHES):
                mm.transpose(bank(k, 0, 128), arena1[:, 128 * k:128 * k + 128], ident)
            mm.transpose(bank(5, 0, 128), arena1[:, 640:768], ident)
            mm.transpose(bank(6, 0, 8), arena1[0:8, 768:896], ident[0:8, 0:8])
            for j in range(XBLK):
                mm.transpose(bank(6, 16 + 16 * j, 32 + 16 * j), arena1[0:16, 1024 + 128 * j:1152 + 128 * j],
                             ident[0:16, 0:16])
            mm.matmul(bank(7, 0, V_COLS), ones[0:1, :], vrow[0:1, :], start=True, stop=True)
            barrier(pe, 1)
            barrier(pe, 2)
            mm.matmul(bank(0, 0, 64), posw_t[0:64, :], const[0:64, C_POS:C_POS + 64], start=True, stop=True)
            mm.matmul(bank(1, 0, 64), posw_t[64:128, :], const[64:128, C_POS:C_POS + 64], start=True, stop=True)
            for n in range(3, SETUP_BARS):
                barrier(pe, n)

        SCAN_STEPS = 7

        def pe_prep(pe, b):
            mm = nc.tensor
            bar(pe, b, 0)
            bar(pe, b, 1)
            bar(pe, b, 2)
            for q in range(TPD):
                for d in range(DIRS):
                    mm.matmul(ps[32 * d:32 * d + 32, 512 * q:512 * q + 512], wdt[:, 32 * d:32 * d + 32],
                              seq[:, d, 512 * q:512 * q + 512], start=True, stop=True)
            bar(pe, b, 3)
            bar(pe, b, 4)
            pe.wait_ge(S["scan_step"], SCAN_STEPS * b + 1)
            for j in range(NCHUNK):
                last = mm.transpose(ps[:, 128 * j:128 * j + 128], work1[:, 128 * j:128 * j + 128], ident)
            last.then_inc(S["dt_turned"], 1)
            bar(pe, b, 5)
            for j in range(NCHUNK):
                mm.transpose(ps[:, 128 * j:128 * j + 128], work2[:, 128 * j:128 * j + 128], ident)
            bar(pe, b, 6)
            bar(pe, b, 7)
            for q in range(2):
                mm.matmul(bank(q), const[:, C_LAST:C_LAST + 128], wdt_tok[:, 512 * q:512 * q + 512],
                          start=True, stop=True)
            for n in range(8, 13):
                bar(pe, b, n)

        def pe_body(pe, b, t, odd):
            mm = nc.tensor
            i = t + 1
            for c in range(CPT):
                if c == 0 and alive(t - 2):
                    pe.wait_ge(S["sqs_ready"], CPT * tile_no(b, t - 1))
                    pe.wait_ge(S["xbg_ready"], chunk_no(b, t, 0) if alive(t - 1) else chunk_no(b, t - 1, 0))
                    for j in range(CPT):
                        last = mm.matmul(bank(B_T, 448 + j, 449 + j), ssum[:, CHUNK * j:CHUNK * j + CHUNK],
                                         ones[:, 0:1], start=True, stop=True)
                    last.then_inc(S["ss_ready"], 1)
                if c == 1 and alive(t - 2):
                    pe.wait_ge(S["r_ready"], tile_no(b, t - 2) + 1)
                    pe.wait_ge(S["s_upd"], chunk_no(b, t, 0) if alive(t - 1) else chunk_no(b, t - 1, 0))
                    for j in range(CPT):
                        last = mm.matmul(bank(B_S, CHUNK * j, CHUNK * j + CHUNK),
                                         rms[:, j:j + 1].broadcast_to([128, 128]), ident, start=True, stop=True)
                    last.then_inc(S["rbc_mm"], 1)
                if alive(t):
                    chunk_head(pe, b, t, c, slot(odd, c))
                tb, cb = lagged(t, c, 1)
                if alive(tb):
                    if c == 1 and alive(t - 2):
                        pe.wait_ge(S["rbc_ready"], tile_no(b, t - 2) + 1)
                    chunk_tail(pe, b, tb, cb, slot(odd, c, 1))
                if c == 0:
                    if alive(t - 2):
                        pe.wait_ge(S["wo_loaded"], 16 * tile_no(b, t - 2) + 16)
                        p_wait(pe, b, i, "out")
                        for m in range(2):
                            last = mm.matmul(bank(B_PX), wo[:, 128 * m:128 * m + 128],
                                             ygs[odd][:, TILE * m:TILE * m + TILE],
                                             start=(m == 0), stop=(m == 1))
                        last.then_inc(S["out_ready"], 1)
                    project_z(pe, b, i, t, 0)
                if c > 0:
                    project_xbc(pe, b, i, i + 1, c - 1, 1 - odd)
                if c == 1:
                    spread_cs(pe, b, i, t, 1)
                if c == 2:
                    project_z(pe, b, i, t, 1)
                if c == 3:
                    spread_cs(pe, b, i, i, 0)

        def project_xbc(pe, b, i, tile, j, half):
            if not alive(tile):
                return
            n = tile_no(b, tile)
            if j == 0:
                pe.wait_ge(S["wx_loaded"], 16 * n + 16)
            p_wait(pe, b, i, "xbc", j)
            nc.tensor.matmul(bank(B_PX), wx[:, half * CONV + 128 * j:half * CONV + 128 * j + 128],
                             useq[:, bass.ds(tile * TILE, TILE)], start=True, stop=True)\
                .then_inc(S["xbc_ready"], 1)

        def project_z(pe, b, i, tile, pair):
            if not alive(tile):
                return
            n = tile_no(b, tile)
            if pair == 0:
                pe.wait_ge(S["wz_loaded"], 16 * n + 16)
            p_wait(pe, b, i, "z", pair)
            for m in range(2):
                last = nc.tensor.matmul(bank(B_PZ, 256 * m, 256 * m + 256), wz[:, 128 * m:128 * m + 128],
                                        useq[:, bass.ds(tile * TILE + 256 * pair, 256)], start=True, stop=True)
            last.then_inc(S["z_ready"], 1)

        def spread_cs(pe, b, i, tile, pair):
            if not alive(tile):
                return
            p_wait(pe, b, i, "e", pair)
            d = tile // TPD
            for m in range(2):
                last = nc.tensor.matmul(bank(B_PZ, 256 * m, 256 * m + 256),
                                        sel_e[:, bass.ds(d * INNER + 128 * m, 128)],
                                        csp[:, bass.ds(tile % TPD * TILE + 256 * pair, 256)],
                                        start=True, stop=True)
            last.then_inc(S["e_ready"], 1)

        def chunk_head(pe, b, t, c, at):
            mm = nc.tensor
            k = chunk_no(b, t, c)
            pe.wait_ge(S["silu_done"], k + 1)
            earlier(pe, "xbg_ready", b, t, c, 1)
            for j in range(2):
                mm.transpose(bank(B_T, 128 * j, 128 * j + 128), xs_of(at)[:, j, :], ident)
            mm.transpose(bank(B_T, 256, 320), xs_of(at)[0:64, 2, :], ident[0:64, 0:64])
            mm.matmul(bank(B_T, 320, 448), xs_of(at)[0:64, 2, :], c_of(at),
                      start=True, stop=True).then_inc(S["tbank_ready"], 1)
            earlier(pe, "l_ready", b, t, c, 1)
            d = t // TPD
            cols = csp[:, bass.ds(t % TPD * TILE + c * CHUNK, CHUNK)]
            for q in range(2):
                for h in range(4):
                    mm.matmul(bank(B_D + q, 128 * h, 128 * h + 128),
                              sel[:, bass.ds(d * HEADS + 4 * q + h, 1)].broadcast_to([128, 128]), cols,
                              start=(h == 0), stop=False, skip_group_check=True)
                mm.matmul(bank(B_D + q), ident_b[:, :], later[:, :].unsqueeze(1).broadcast_to([128, 4, 128]),
                          start=False, stop=False, skip_group_check=True)
                last = mm.matmul(bank(B_D + q), cols,
                                 neg[:, bass.ds(d * HEADS + 4 * q, 4)].unsqueeze(2).broadcast_to([128, 4, 128]),
                                 start=False, stop=True, skip_group_check=True)
            last.then_inc(S["d_ready"], 1)

        def chunk_tail(pe, b, t, c, at):
            mm = nc.tensor
            k = chunk_no(b, t, c)
            pe.wait_ge(S["x_ready"], k + 1)
            earlier(pe, "s_upd", b, t, c, 1)
            for m in range(2):
                last = mm.matmul(bank(B_S, 0, CHUNK)[64 * m:64 * m + 64],
                                 buf(xbg, c, 448)[:, 256:320], buf(xw, c, INNER)[:, 128 * m:128 * m + 128],
                                 start=True, stop=True)
            last.then_inc(S["st_ready"], 1)
            pe.wait_ge(S["m_ready"], k + 1)
            earlier(pe, "ysum_done", b, t, c, 1)
            for h in range(HEADS):
                q = h % 4
                mm.matmul(ps[32 * q:32 * q + 32, 512 * (B_Y + h // 4):512 * (B_Y + h // 4) + CHUNK],
                          buf(xdt, c, INNER)[:, HEAD * h:HEAD * h + HEAD], mix[:, c % 2, h, :],
                          start=True, stop=True)
            mm.matmul(bank(B_Y, 128, 256), buf(st, c, CHUNK)[0:64, :], c_of(at),
                      start=True, stop=True)
            mm.matmul(bank(B_Y + 1, 128, 256), buf(st, c, CHUNK)[64:128, :], xs_of(at)[64:128, 2, :],
                      start=True, stop=True).then_inc(S["b_done"], 1)

        def image_rows(d, q):
            v = seq[:, d, :].rearrange("p (a b) -> p a b", b=64)
            if d == 0:
                return [(v[:, 8 * q:8 * q + 8, :], slice(0, 8), slice(0, 64))]
            if d == 1:
                return [(v[:, :, 8 * q:8 * q + 8].rearrange("p w h -> p h w"), slice(0, 8), slice(0, 64))]
            if d == 2:
                return [(v[:, 8 * q:8 * q + 8:2, :], slice(0, 8, 2), slice(0, 64)),
                        (v[:, 8 * q + 1:8 * q + 8:2, ::-1], slice(1, 8, 2), slice(0, 64))]
            hi, lo = 63 - 8 * q, 63 - 8 * q - 8
            back = v[:, 1::2, hi:lo:-1] if lo >= 0 else v[:, 1::2, hi::-1]
            return [(v[:, 0::2, 8 * q:8 * q + 8].rearrange("p w h -> p h w"), slice(0, 8), slice(0, 64, 2)),
                    (back.rearrange("p w h -> p h w"), slice(0, 8), slice(1, 64, 2))]

        POST = 14

        def step(eng, b, n):
            eng.wait_ge(S["post_step"], POST * b + n)

        def pe_post(pe, b):
            mm = nc.tensor
            bar(pe, b, 13)
            step(pe, b, 1)
            mm.matmul(bank(4, 0, BRANCHES), ones[:, :], small[:, 0:5], start=True, stop=True)\
                .then_inc(S["post_step"], 1)
            for q in range(TPD):
                o = bank(q % 4).rearrange("p (h w) -> p h w", w=64)
                n = TPD * b + q
                if q >= 4:
                    pe.wait_ge(S["proj_evac"], n - 3)
                for d in range(DIRS):
                    for src, rows, cols in image_rows(d, q):
                        mm.matmul(o[:, rows, cols], pw_t[:, 128 * (d + 1):128 * (d + 2)], src,
                                  start=(d == 0), stop=False, skip_group_check=True)
                mm.matmul(bank(q % 4), pw_t[:, 0:128], local[:, 512 * q:512 * q + 512], start=False, stop=True,
                          skip_group_check=True).then_inc(S["proj_ready"], 1)
            step(pe, b, 9)
            mm.matmul(bank(5, 0, 1), const[:, C_GROUP:C_GROUP + 128], small[:, 20:21], start=True, stop=True)\
                .then_inc(S["post_step"], 1)
            step(pe, b, 12)
            mm.matmul(bank(6, 0, 1), const[:, C_GROUP:C_GROUP + 128], small[:, 24:25], start=True, stop=True)\
                .then_inc(S["post_step"], 1)
            bar(pe, b, 14)

        def pe_program(pe):
            pe_setup(pe)
            with pe.Fori(0, BATCH) as b:
                pe_prep(pe, b)
                run_tiles(pe, b, pe_body)
                pe_post(pe, b)

        def act_setup(act):
            barrier(act, 0)
            barrier(act, 1)
            barrier(act, 2)
            barrier(act, 3)
            barrier(act, 4)
            act.activation(small[:, 43:44], small[:, 41:42], ACT.Exp)
            barrier(act, 5)
            barrier(act, 6)

        def act_prep(act, b):
            bar(act, b, 0)
            bar(act, b, 1)
            img = seq[:, 0, :].rearrange("p (h w) -> p h w", w=64)
            act.activation(seq[:, 1, :].rearrange("p (w h) -> p h w", h=64), img, ACT.Copy)
            for pick, dst in order_parts(2) + order_parts(3)[:1]:
                act.activation(dst, pick(seq[:, 0, :]), ACT.Copy)
            bar(act, b, 2)
            bar(act, b, 3)
            P_ = S["prep_step"]
            act.activation(work1, ps[:, :], ACT.Abs, bias=dirpar[:, 1:2]).then_inc(P_, 1)
            act.activation(work2, ps[:, :], ACT.Relu, bias=dirpar[:, 1:2])
            act.wait_ge(P_, 3 * b + 1)
            act.activation(work1, work1, ACT.Exp, scale=-1.0).then_inc(P_, 1)
            act.wait_ge(P_, 3 * b + 2)
            act.activation(work1, work1, ACT.Ln, bias=1.0).then_inc(P_, 1)
            bar(act, b, 4)
            act.activation(local[:, :], local[:, :], ACT.Gelu_apprx_tanh, accum_out=sums[:, 0:1])
            act.wait_ge(S["dt_turned"], b + 1)
            tok = ps[:, :].rearrange("p (j d r h) -> p j d r h", j=NCHUNK, d=DIRS, r=REP)
            for d in range(DIRS):
                act.activation(tab_view(dt_tok)[:, d], tok[:, :, d, 0, :], ACT.Copy)
            bar(act, b, 5)
            bar(act, b, 6)
            for d in range(DIRS):
                act.activation(tab_view(wdt_tok)[:, d], tok[:, :, d, 0, :], ACT.Copy)
            bar(act, b, 7)
            bar(act, b, 8)
            for m in range(2):
                half = slice(64 * m, 64 * m + 64)
                act.activation(dec_bc[half, :].rearrange("p (k h) -> p k h", h=4),
                               ps[half, 0:1024].rearrange("p (k h) -> p k h", h=HEADS)[:, :, 4 * m:4 * m + 4], ACT.Exp)
            bar(act, b, 9)
            bar(act, b, 10)
            act.activation(wdt_tok[:, :], wdt_tok[:, :], ACT.Exp)
            bar(act, b, 11)
            bar(act, b, 12)

        def tab_view(tab):
            return tab[:, :].rearrange("p (d j h) -> p d j h", d=DIRS, j=NCHUNK)

        def act_body(act, b, t, odd):
            i = t + 1
            for c in range(CPT):
                if c == 0 and alive(t - 2):
                    n = tile_no(b, t - 2)
                    act.wait_ge(S["ss_ready"], n + 1)
                    if alive(t):
                        act.wait_ge(S["tbank_ready"], chunk_no(b, t, 0) + 1)
                    if not first(t - 2):
                        act.wait_ge(S["r_ready"], n)
                    act.activation(var[:, :], bank(B_T, 448, 448 + CPT), ACT.Copy, scale=1.0 / INNER)\
                        .then_inc(S["ss_evac"], 1)
                k = chunk_no(b, t, c)
                if c == 1 and alive(t - 2):
                    n = tile_no(b, t - 2)
                    act.wait_ge(S["rbc_mm"], n + 1)
                    if not first(t - 2):
                        act.wait_ge(S["o_evac"], n)
                    act.activation(rbc[:, :], bank(B_S), ACT.Copy).then_inc(S["rbc_ready"], 1)
                if alive(t):
                    act.wait_ge(S["tbank_ready"], k + 1)
                    earlier(act, "x_ready", b, t, c, 2)
                    earlier(act, "st_ready", b, t, c, 2)
                    earlier(act, "m_ready", b, t, c, 2)
                    act.activation(buf(xbg, c, 448), bank(B_T, 0, 448), ACT.Copy).then_inc(S["xbg_ready"], 1)
                if alive(t):
                    act.wait_ge(S["d_ready"], k + 1)
                    act.activation(decay[:, c % 2].rearrange("p h t -> p (h t)"), ps[:, 512 * B_D:512 * B_D + 1024],
                                   ACT.Exp).then_inc(S["l_ready"], 1)
                if c < 2:
                    first_tap(act, b, i, c + 1)
                tq, cq = lagged(t, c, 3)
                if alive(tq):
                    act.wait_ge(S["yg_ready"], chunk_no(b, tq, cq) + 1)
                    earlier(act, "sqs_ready", b, tq, cq, 2)
                    sl = slice(CHUNK * cq, CHUNK * cq + CHUNK)
                    act.activation(two(buf(sq, cq, INNER)),
                                   two(ygs[odd if c >= 3 else 1 - odd][:, :])[:, :, sl], ACT.Square)\
                        .then_inc(S["sq_ready"], 1)
                if c < XBLK and alive(i):
                    n = tile_no(b, i)
                    act.wait_ge(S["conv_done"], 3 * n + c + 1)
                    if not first(i):
                        act.wait_ge(S["silu_done"], CPT * n)
                    act.activation(tanh[:, c, :], conv[:, c, :], ACT.Tanh).then_inc(S["tanh_done"], 1)
                if c > 0:
                    evac_xbc(act, b, i + 1, c - 1)
                if c == 0:
                    tanh_z(act, b, t, 0)
                if c == 1:
                    exp_cs(act, b, t, 1)
                if c == 2:
                    tanh_z(act, b, t, 1)
                if c == 3:
                    exp_cs(act, b, i, 0)

        def evac_xbc(act, b, i, j):
            if not alive(i):
                return
            n = tile_no(b, i)
            act.wait_ge(S["xbc_ready"], 3 * n + j + 1)
            if not first(i):
                act.wait_ge(S["conv_done"], 3 * n + j - 2)
            act.activation(raw[:, j, 3:3 + TILE], bank(B_PX), ACT.Copy).then_inc(S["xbc_evac"], 1)

        def first_tap(act, b, i, j):
            if not alive(i):
                return
            n = XBLK * tile_no(b, i) + j
            if not first(i):
                act.wait_ge(S["silu_done"], CPT * tile_no(b, i))
            act.wait_ge(S["xbc_evac"], n + 1)
            act.activation(conv[:, j, :], raw[:, j, 0:TILE], ACT.Copy,
                           scale=taps[:, bass.ds(i // TPD * XBLK * TAPS + j * TAPS, 1)]).then_inc(S["first_tap"], 1)

        def tanh_z(act, b, tile, pair):
            if not alive(tile):
                return
            n = tile_no(b, tile)
            act.wait_ge(S["z_ready"], 2 * n + pair + 1)
            if not (first(tile) and pair == 0):
                act.wait_ge(S["gate_done"], 2 * n + pair)
            act.activation(thz[:, :], bank(B_PZ), ACT.Tanh, scale=0.5).then_inc(S["thz_ready"], 1)

        def exp_cs(act, b, tile, pair):
            if not alive(tile):
                return
            n = tile_no(b, tile)
            act.wait_ge(S["e_ready"], 2 * n + pair + 1)
            if not first(tile):
                act.wait_ge(S["y1_done"], CPT * n - CPT + 2 * pair + 2)
            act.activation(ecs[:, TILE * pair:TILE * pair + TILE], bank(B_PZ), ACT.Exp).then_inc(S["ecs_ready"], 1)

        def act_post(act, b):
            bar(act, b, 13)
            step(act, b, 4)
            act.activation(small[:, 8:10], small[:, 8:10], ACT.Gelu_apprx_tanh).then_inc(S["post_step"], 1)
            step(act, b, 6)
            act.activation(small[:, 12:17], small[:, 12:17], ACT.Tanh, scale=0.5).then_inc(S["post_step"], 1)
            for q in range(TPD):
                act.wait_ge(S["proj_ready"], TPD * b + q + 1)
                act.activation(work1[:, 512 * q:512 * q + 512], bank(q % 4), ACT.Copy).then_inc(S["proj_evac"], 1)
            step(act, b, 14)
            for q in range(4):
                act.activation(work1[:, 1024 * q:1024 * q + 1024], work1[:, 1024 * q:1024 * q + 1024],
                               ACT.Gelu_apprx_tanh, scale=small[:, 28:29], bias=small[:, 29:30])\
                    .then_inc(S["stat_step"], 1)
            bar(act, b, 14)

        def act_program(act):
            act_setup(act)
            with act.Fori(0, BATCH) as b:
                act_prep(act, b)
                run_tiles(act, b, act_body)
                act_post(act, b)

        def dve_setup(dve):
            v = nc.vector
            v.memset(ones[:, :], 1.0)
            v.memset(small[:, 32:64], -0.5)
            v.memset(half_pow[:, :], -0.5)
            v.memset(st[:, :], 0.0)
            barrier(dve, 0)
            barrier(dve, 1)
            v.tensor_copy(pw_t[:, :].rearrange("p (k o) -> p k o", k=BRANCHES),
                          ps[:, 0:BRANCHES * 512].rearrange("p (k o) -> p k o", k=BRANCHES)[:, :, 0:128])
            v.tensor_copy(posw_t[:, :], bank(5, 0, 128))
            v.tensor_copy(nw_t[:, :], bank(6, 0, 8))
            v.tensor_scalar(taps[:, :].rearrange("p (d j k) -> p d j k", d=DIRS, j=XBLK),
                            bank(6, 16, 64).rearrange("p (j d k) -> p d j k", j=XBLK, d=DIRS), 0.5, None, ALU.mult)
            v.tensor_copy(vbc[:, :], bank(7, 0, V_COLS))
            for q in range(4):
                rows = slice(32 * q, 32 * q + 32)
                v.tensor_copy(d_col[rows, :], ps[rows, 512 * 7 + V_DP + q:512 * 7 + V_DP + 32:4])
            v.tensor_copy(wdt[:, :].rearrange("p (d r h) -> p d r h", d=DIRS, r=REP),
                          small[:, 0:32].rearrange("p (d h) -> p d h", d=DIRS).unsqueeze(2)
                          .broadcast_to([128, DIRS, REP, HEADS]))
            v.tensor_copy(ident_b[:, :], ident)
            v.tensor_copy(later[:, :], const[:, C_TRI:C_TRI + 128])
            v.tensor_copy(neg[:, :], const[:, C_NEG:C_NEG + 32])
            v.tensor_copy(sel[:, :], const[:, C_SEL:C_SEL + 32])
            v.tensor_copy(sel_e[:, :].rearrange("p (n s) -> p n s", s=HEAD),
                          const[:, C_SEL:C_SEL + 32].unsqueeze(2).broadcast_to([128, 32, HEAD]))
            barrier(dve, 2)
            v.tensor_tensor(arena2[:, 0:32], vbc[:, V_ALOG:V_ALOG + 32], const[:, C_SEL:C_SEL + 32], ALU.mult)
            v.tensor_tensor(arena2[:, 32:64], vbc[:, V_DTB:V_DTB + 32], const[:, C_SEL:C_SEL + 32], ALU.mult)
            for d in range(DIRS):
                for m in range(2):
                    w = wo_all[:, (2 * d + m) * CH:(2 * d + m + 1) * CH]
                    v.tensor_scalar(w, w, nw_t[:, 2 * d + m:2 * d + m + 1], None, ALU.mult)
            barrier(dve, 3)
            v.reduce_sum(small[:, 41:42], arena2[:, 0:32], AX_X)
            v.reduce_sum(dirpar[:, 1:2], arena2[:, 32:64], AX_X)
            v.tensor_copy(pos[:, 0:64], bank(0, 0, 64))
            v.tensor_copy(pos[:, 64:128], bank(1, 0, 64))
            barrier(dve, 4)
            barrier(dve, 5)
            v.tensor_tensor(dirpar[:, 0:1], small[:, 43:44], const[:, C_GE0:C_GE0 + 1], ALU.mult)
            barrier(dve, 6)

        def dve_prep(dve, b):
            v = nc.vector
            bar(dve, b, 0)
            img = seq[:, 0, :].rearrange("p (h w) -> p h w", w=64)
            LS = S["local_step"]
            n_local = 11
            v.tensor_tensor(img, img, pos[:, 0:64].unsqueeze(2).broadcast_to([128, 64, 64]), ALU.add).then_inc(LS, 1)
            dve.wait_ge(LS, n_local * b + 1)
            v.tensor_tensor(img, img, pos[:, 64:128].unsqueeze(1).broadcast_to([128, 64, 64]), ALU.add)\
                .then_inc(LS, 1)
            bar(dve, b, 1)
            acc = local[:, :].rearrange("p (h w) -> p h w", w=64)
            v.tensor_scalar(acc, img, lw[:, 4:5], None, ALU.mult).then_inc(LS, 1)
            n = 3
            for dh in (-1, 0, 1):
                for dw in (-1, 0, 1):
                    if dh == 0 and dw == 0:
                        continue
                    h0, h1 = max(0, -dh), 64 - max(0, dh)
                    w0, w1 = max(0, -dw), 64 - max(0, dw)
                    at = 3 * (dh + 1) + dw + 1
                    dve.wait_ge(LS, n_local * b + n)
                    v.scalar_tensor_tensor(acc[:, h0:h1, w0:w1], img[:, h0 + dh:h1 + dh, w0 + dw:w1 + dw],
                                           lw[:, at:at + 1], acc[:, h0:h1, w0:w1], ALU.mult, ALU.add)\
                        .then_inc(LS, 1)
                    n += 1
                    if n == 5:
                        bar(dve, b, 2)
                    if n == 7:
                        bar(dve, b, 3)
            v.memset(sums[:, 1:TPD], 0.0)
            bar(dve, b, 4)
            SC = S["scan_step"]
            n_scan = SCAN_STEPS
            v.tensor_tensor(work1, work1, work2, ALU.add).then_inc(SC, 1)
            dve.wait_ge(SC, n_scan * b + 1)
            v.tensor_scalar(work2, work1, dirpar[:, 0:1], None, ALU.mult).then_inc(SC, 1)
            dve.wait_ge(SC, n_scan * b + 2)
            for j in range(NCHUNK):
                w = work2[:, 128 * j:128 * j + 128]
                v.tensor_tensor_scan(w, ones[:, :], w, 0.0, ALU.mult, ALU.add)
            bar(dve, b, 5)
            v.tensor_copy(csp[:, :], work2).then_inc(SC, 1)
            bar(dve, b, 6)
            v.scalar_tensor_tensor(work2, csp[:, :], const[:, C_GE1:C_GE1 + 1], work2, ALU.mult, ALU.add)\
                .then_inc(SC, 1)
            dve.wait_ge(SC, n_scan * b + 4)
            v.tensor_copy(csp[:, :], work2).then_inc(SC, 1)
            bar(dve, b, 7)
            bar(dve, b, 8)
            bar(dve, b, 9)
            v.tensor_tensor(wdt_tok[:, :], ps[:, 0:1024], wdt_tok[:, :], ALU.subtract)
            bar(dve, b, 10)
            dve.wait_ge(SC, n_scan * b + 5)
            v.scalar_tensor_tensor(work2, csp[:, :], const[:, C_GE2:C_GE2 + 1], work2, ALU.mult, ALU.add)\
                .then_inc(SC, 1)
            bar(dve, b, 11)
            v.tensor_tensor(wdt_tok[:, :], wdt_tok[:, :], dt_tok[:, :], ALU.mult).then_inc(S["wdt_step"], 1)
            dve.wait_ge(SC, n_scan * b + 6)
            v.tensor_copy(csp[:, :], work2).then_inc(SC, 1)
            dve.wait_ge(S["wdt_step"], b + 1)
            v.memset(tab_view(wdt_tok)[:, :, NCHUNK - 1, :], 0.0)
            v.memset(dec_bc[:, :].rearrange("p (d j h) -> p d j h", d=DIRS, h=4)[:, :, NCHUNK - 1, :], 0.0)
            dve.wait_ge(SC, n_scan * b + 7)
            v.memset(raw[:, :, 0:3], 0.0)
            bar(dve, b, 12)

        def dve_body(dve, b, t, odd):
            i = t + 1
            for c in range(CPT):
                tb, cb = lagged(t, c, 1)
                if c == 0:
                    tap(dve, b, i, c, 0)
                if c < XBLK:
                    tap(dve, b, i, c, 1)
                else:
                    silu(dve, b, i, 0, odd)
                    silu(dve, b, i, 1, odd)
                if c == 1:
                    scale_out(dve, b, t - 2)
                carry_state(dve, b, tb, cb)
                if c < XBLK:
                    tap(dve, b, i, c, 2)
                if c == 1:
                    gate_z(dve, b, t, 0)
                if c == 3:
                    gate_z(dve, b, t, 1)
                y_carried(dve, b, tb, cb)
                if c < XBLK:
                    tap(dve, b, i, c, 3)
                else:
                    silu(dve, b, i, 2, odd)
                y_sum(dve, b, tb, cb)
                if c < XBLK:
                    keep_tail(dve, b, i, c)
                else:
                    silu(dve, b, i, 3, odd)
                mix_chunk(dve, b, t, c)

        def carry_state(dve, b, t, c):
            if not alive(t):
                return
            k = chunk_no(b, t, c)
            dve.wait_ge(S["st_ready"], k + 1)
            dve.wait_ge(S["sdec_ready"], k + 1)
            earlier(dve, "b_done", b, t, c, 1)
            nc.vector.tensor_tensor(buf(st, c + 1, CHUNK), bank(B_S, 0, CHUNK), st_dec[:, :], ALU.add)\
                .then_inc(S["s_upd"], 1)

        def mix_chunk(dve, b, t, c):
            if not alive(t):
                return
            dve.wait_ge(S["l_ready"], chunk_no(b, t, c) + 1)
            earlier(dve, "b_done", b, t, c, 2)
            nc.vector.tensor_tensor(mix[:, c % 2], decay[:, c % 2],
                                    buf(xbg, c, 448)[:, 320:448].unsqueeze(1).broadcast_to([128, HEADS, CHUNK]),
                                    ALU.mult).then_inc(S["m_ready"], 1)

        def y_carried(dve, b, t, c):
            if not alive(t):
                return
            dve.wait_ge(S["ecs_ready"], 2 * tile_no(b, t) + c // 2 + 1)
            dve.wait_ge(S["b_done"], chunk_no(b, t, c) + 1)
            earlier(dve, "ysum_done", b, t, c, 1)
            nc.vector.tensor_tensor(two(y1[:, :]), y_banks[:, :, 128:256], pair_of(ecs, c), ALU.mult)\
                .then_inc(S["y1_done"], 1)

        def y_sum(dve, b, t, c):
            if not alive(t):
                return
            earlier(dve, "yg_ready", b, t, c, 2)
            dve.wait_ge(S["y1_done"], chunk_no(b, t, c) + 1)
            nc.vector.tensor_tensor(two(buf(y2, c, INNER)), y_banks[:, :, 0:128], two(y1[:, :]), ALU.add)\
                .then_inc(S["ysum_done"], 1)

        def scale_out(dve, b, tile):
            if not alive(tile):
                return
            n = tile_no(b, tile)
            dve.wait_ge(S["out_ready"], n + 1)
            dve.wait_ge(S["rbc_ready"], n + 1)
            nc.vector.scalar_tensor_tensor(useq[:, bass.ds(tile * TILE, TILE)], bank(B_PX), 1.0, rbc[:, :],
                                           ALU.mult, ALU.mult, accum_out=sums[:, bass.ds(TPD + tile, 1)])\
                .then_inc(S["o_evac"], 1)

        def tap(dve, b, i, j, k):
            if not alive(i) or (k == 0 and j > 0):
                return
            v = nc.vector
            n = XBLK * tile_no(b, i) + j
            w = taps[:, bass.ds(i // TPD * XBLK * TAPS + j * TAPS + k, 1)]
            if k == 0:
                dve.wait_ge(S["xbc_evac"], n + 1)
                if not first(i):
                    dve.wait_ge(S["conv_done"], n - 2)
                    dve.wait_ge(S["silu_done"], CPT * tile_no(b, i))
                v.tensor_scalar(conv[:, j, :], raw[:, j, 0:TILE], w, None, ALU.mult).then_inc(S["tap_done"], 1)
                return
            if k == 1 and j > 0:
                dve.wait_ge(S["first_tap"], 2 * tile_no(b, i) + j)
            else:
                taps_before = (0, TAPS - 1, 2 * TAPS - 2)[j]
                dve.wait_ge(S["tap_done"], (3 * TAPS - 2) * tile_no(b, i) + taps_before + k)
            v.scalar_tensor_tensor(conv[:, j, :], raw[:, j, k:k + TILE], w, conv[:, j, :],
                                   ALU.mult, ALU.add).then_inc(S["tap_done"], 1)

        def keep_tail(dve, b, i, j):
            if not alive(i):
                return
            nc.vector.tensor_scalar(raw[:, j, 0:3], raw[:, j, TILE:TILE + 3],
                                    const[:, bass.ds(C_FLAG + i + 1, 1)], None, ALU.mult)\
                .then_inc(S["conv_done"], 1)

        def gate_z(dve, b, tile, pair):
            if not alive(tile):
                return
            n = tile_no(b, tile)
            dve.wait_ge(S["thz_ready"], 2 * n + pair + 1)
            if not first(tile):
                dve.wait_ge(S["yg_ready"], CPT * n - CPT + 2 * pair + 2)
            nc.vector.scalar_tensor_tensor(gate[:, TILE * pair:TILE * pair + TILE], thz[:, :], 1.0, bank(B_PZ),
                                           ALU.add, ALU.mult).then_inc(S["gate_done"], 1)

        def silu(dve, b, i, c, odd):
            if not alive(i):
                return
            v = nc.vector
            dve.wait_ge(S["tanh_done"], 3 * tile_no(b, i) + 3)
            if not isinstance(i, int) or i >= 2:
                k = chunk_no(b, i, c) - 2 * CPT
                dve.wait_ge(S["tbank_ready"], k + 1)
                dve.wait_ge(S["x_ready"], k + 1)
                dve.wait_ge(S["b_done"], k + 1)
            cols = slice(128 * c, 128 * c + 128)
            v.scalar_tensor_tensor(xs_of(slot(odd, c, -CPT)), tanh[:, :, cols], 1.0, conv[:, :, cols], ALU.add, ALU.mult)
            v.scalar_tensor_tensor(c_of(slot(odd, c, -CPT)), tanh[64:128, 2, cols], 1.0, conv[64:128, 2, cols],
                                   ALU.add, ALU.mult).then_inc(S["silu_done"], 1)

        def order_parts(d):
            im = lambda x: x.rearrange("p (h w) -> p h w", w=64)
            s = seq[:, d, :].rearrange("p (a b) -> p a b", b=64)
            if d == 0:
                return [(lambda x: im(x), s)]
            if d == 1:
                return [(lambda x: im(x), s.rearrange("p w h -> p h w"))]
            if d == 2:
                return [(lambda x: im(x)[:, 0::2, :], s[:, 0::2, :]),
                        (lambda x: im(x)[:, 1::2, :], s[:, 1::2, ::-1])]
            return [(lambda x: im(x)[:, :, 0::2].rearrange("p h w -> p w h"), s[:, 0::2, :]),
                    (lambda x: im(x)[:, :, 1::2].rearrange("p h w -> p w h"), s[:, 1::2, ::-1])]

        def dve_post(dve, b):
            v = nc.vector
            bar(dve, b, 13)
            P_ = S["post_step"]
            v.reduce_sum(small[:, 0:5], sums[:, :].rearrange("p (k t) -> p k t", k=BRANCHES), AX_X).then_inc(P_, 1)
            step(dve, b, 2)
            w1 = vbc[:, V_W1:V_W1 + 10].rearrange("p (i j) -> p j i", j=2)
            desc = bank(4, 0, BRANCHES).unsqueeze(1).broadcast_to([128, 2, BRANCHES])
            v.scalar_tensor_tensor(small[:, 44:54].rearrange("p (j i) -> p j i", j=2), desc, 1.0 / (CH * PIX), w1,
                                   ALU.mult, ALU.mult).then_inc(P_, 1)
            step(dve, b, 3)
            SS = S["fuse_step"]
            n_fuse = 8
            v.reduce_sum(small[:, 6:8], small[:, 44:54].rearrange("p (j i) -> p j i", j=2), AX_X).then_inc(SS, 1)
            dve.wait_ge(SS, n_fuse * b + 1)
            v.tensor_tensor(small[:, 8:10], small[:, 6:8], vbc[:, V_B1:V_B1 + 2], ALU.add).then_inc(P_, 1)
            step(dve, b, 5)
            w2 = vbc[:, V_W2:V_W2 + 10].rearrange("p (j i) -> p i j", j=2)
            v.tensor_tensor(small[:, 44:54].rearrange("p (i j) -> p i j", j=2),
                            small[:, 8:10].unsqueeze(1).broadcast_to([128, BRANCHES, 2]), w2, ALU.mult).then_inc(SS, 1)
            dve.wait_ge(SS, n_fuse * b + 2)
            v.reduce_sum(small[:, 54:59], small[:, 44:54].rearrange("p (i j) -> p i j", j=2), AX_X).then_inc(SS, 1)
            dve.wait_ge(SS, n_fuse * b + 3)
            v.tensor_tensor(small[:, 12:17], small[:, 54:59], vbc[:, V_B2:V_B2 + 5], ALU.add).then_inc(P_, 1)
            step(dve, b, 7)
            v.tensor_scalar(small[:, 12:17], small[:, 12:17], 0.5, 0.5, ALU.mult, ALU.add).then_inc(P_, 1)
            dve.wait_ge(S["x_loaded"], 32 * b + 32)
            step(dve, b, 8)
            FS = S["branch_added"]
            n = 0
            v.scalar_tensor_tensor(work2, local[:, :], small[:, 12:13], work2, ALU.mult, ALU.add).then_inc(FS, 1)
            for d in range(DIRS):
                n += 1
                dve.wait_ge(FS, 5 * b + n)
                for pick, src in order_parts(d):
                    last = v.scalar_tensor_tensor(pick(work2), src, small[:, 13 + d:14 + d], pick(work2),
                                                  ALU.mult, ALU.add)
                last.then_inc(FS, 1)
            stats = gate[:, 0:6 * TPD]
            for q in range(TPD):
                dve.wait_ge(S["proj_evac"], TPD * b + q + 1)
                last = v.bn_stats(stats[:, 6 * q:6 * q + 6], work1[:, 512 * q:512 * q + 512])
            last.then_inc(SS, 1)
            dve.wait_ge(SS, n_fuse * b + 4)
            settle(dve)
            v.bn_aggr(small[:, 20:22], stats).then_inc(P_, 1)
            step(dve, b, 10)
            v.tensor_copy(small[:, 22:23], bank(5, 0, 1)).then_inc(SS, 1)
            dve.wait_ge(SS, n_fuse * b + 5)
            v.tensor_tensor(small[:, 23:24], small[:, 20:21], small[:, 22:23], ALU.subtract).then_inc(P_, 1)
            step(dve, b, 11)
            v.scalar_tensor_tensor(small[:, 24:25], small[:, 23:24], small[:, 23:24], small[:, 21:22],
                                   ALU.mult, ALU.add).then_inc(P_, 1)
            step(dve, b, 13)
            v.tensor_scalar(small[:, 25:26], bank(6, 0, 1), EPS, None, ALU.add).then_inc(SS, 1)
            dve.wait_ge(S["var_done"], (TILES + 1) * b + TILES + 1)
            v.tensor_tensor(small[:, 28:29], small[:, 26:27], gnp[:, 0:1], ALU.mult).then_inc(SS, 1)
            dve.wait_ge(SS, n_fuse * b + 7)
            v.tensor_tensor(small[:, 27:28], small[:, 28:29], small[:, 22:23], ALU.mult).then_inc(SS, 1)
            dve.wait_ge(SS, n_fuse * b + 8)
            v.tensor_tensor(small[:, 29:30], gnp[:, 1:2], small[:, 27:28], ALU.subtract).then_inc(P_, 1)
            dve.wait_ge(FS, 5 * b + 5)
            for q in range(4):
                dve.wait_ge(S["stat_step"], 4 * b + q + 1)
                w = slice(1024 * q, 1024 * q + 1024)
                v.tensor_tensor(work2[:, w], work2[:, w], work1[:, w], ALU.add).then_inc(S["part_ready"], 1)
            bar(dve, b, 14)

        def dve_program(dve):
            dve_setup(dve)
            with dve.Fori(0, BATCH) as b:
                dve_prep(dve, b)
                run_tiles(dve, b, dve_body)
                dve_post(dve, b)

        def pool_setup(pool):
            for n in range(SETUP_BARS):
                barrier(pool, n)

        def pool_prep(pool, b):
            g = nc.gpsimd
            bar(pool, b, 0)
            bar(pool, b, 1)
            pick, dst = order_parts(3)[1]
            g.tensor_copy(dst, pick(seq[:, 0, :]))
            for n in range(2, 13):
                bar(pool, b, n)

        def pool_body(pool, b, t, odd):
            g = nc.gpsimd
            for c in range(CPT):
                ty, cy = lagged(t, c, 2)
                if alive(ty):
                    k = chunk_no(b, ty, cy)
                    pool.wait_ge(S["x_ready"], k + 1)
                    pool.wait_ge(S["ysum_done"], k + 1)
                    y_, xd_ = buf(y2, cy, INNER), buf(xd, cy, INNER)
                    g.tensor_tensor(y_, y_, xd_, ALU.add).then_inc(S["y3_done"], 1)
                    pool.wait_ge(S["gate_done"], 2 * tile_no(b, ty) + cy // 2 + 1)
                    if not first(ty):
                        pool.wait_ge(S["sq_ready"], chunk_no(b, ty, cy) - 3)
                    if not isinstance(ty, int) or ty >= 2:
                        pool.wait_ge(S["out_ready"], tile_no(b, ty) - 1)
                    pool.wait_ge(S["y3_done"], k + 1)
                    yg = two(ygs[odd if c >= 2 else 1 - odd][:, :])
                    g.tensor_tensor(yg[:, :, CHUNK * cy:CHUNK * cy + CHUNK], two(y_), pair_of(gate, cy), ALU.mult).then_inc(S["yg_ready"], 1)
                if alive(t - 1):
                    pool.wait_ge(S["sq_ready"], chunk_no(b, t - 1, c) + 1)
                    if not first(t - 1):
                        pool.wait_ge(S["ss_ready"], tile_no(b, t - 1))
                    sq_ = buf(sq, c, INNER)
                    g.tensor_tensor(ssum[:, CHUNK * c:CHUNK * c + CHUNK], sq_[:, 0:CHUNK], sq_[:, CHUNK:INNER],
                                    ALU.add).then_inc(S["sqs_ready"], 1)
                if c == 0 and alive(t - 2):
                    n = tile_no(b, t - 2)
                    pool.wait_ge(S["ss_evac"], n + 1)
                    settle(pool)
                    g.tensor_scalar(var[:, :], var[:, :], 4 * EPS, None, ALU.add).then_inc(S["var_done"], 1)
                    if not first(t - 2):
                        pool.wait_ge(S["rbc_mm"], n)
                    pool.wait_ge(S["var_done"], n + b + 1)
                    g.tensor_tensor(rms[:, :], var[:, :], half_pow[:, :], ALU.pow).then_inc(S["r_ready"], 1)
                if alive(t):
                    k = chunk_no(b, t, c)
                    earlier(pool, "b_done", b, t, c, 2)
                    pool.wait_ge(S["xbg_ready"], k + 1)
                    settle(pool)
                    x_ = by_head(buf(xbg, c, 448)[:, 0:256])
                    g.tensor_tensor(by_head(buf(xw, c, INNER)), x_, table(wdt_tok, t, c), ALU.mult)
                    g.tensor_tensor(by_head(buf(xdt, c, INNER)), x_, table(dt_tok, t, c), ALU.mult)
                    dp = d_col[:, bass.ds(t // TPD * 2, 2)].unsqueeze(2).broadcast_to([128, 2, CHUNK])
                    earlier(pool, "yg_ready", b, t, c, 2)
                    settle(pool)
                    g.tensor_tensor(two(buf(xd, c, INNER)), xs_of(slot(odd, c))[:, 0:2, :], dp, ALU.mult)\
                        .then_inc(S["x_ready"], 1)
                    earlier(pool, "s_upd", b, t, c, 1)
                    settle(pool)
                    g.tensor_tensor(st_dec[:, :].rearrange("p (h d) -> p h d", h=4),
                                    buf(st, c, CHUNK).rearrange("p (h d) -> p h d", h=4), table(dec_bc, t, c, 4),
                                    ALU.mult).then_inc(S["sdec_ready"], 1)

        def pool_post(pool, b):
            bar(pool, b, 13)
            pool.wait_ge(S["fuse_step"], 8 * b + 6)
            nc.gpsimd.tensor_tensor(small[:, 26:27], small[:, 25:26], small[:, 60:61], ALU.pow)\
                .then_inc(S["var_done"], 1)
            bar(pool, b, 14)

        def pool_program(pool):
            pool_setup(pool)
            with pool.Fori(0, BATCH) as b:
                pool_prep(pool, b)
                run_tiles(pool, b, pool_body)
                pool_post(pool, b)

        block = ctx.enter_context(nc.Block())

        @block.sync
        def _(sp):
            sp_program(sp)

        @block.tensor
        def _(pe):
            pe_program(pe)

        @block.scalar
        def _(act):
            act_program(act)

        @block.vector
        def _(dve):
            dve_program(dve)

        @block.gpsimd
        def _(pool):
            pool_program(pool)


_INS = ["x", "L0_conv_pos_proj_w", "L0_conv_local_w", "L0_conv_W_in", "L0_conv_conv_w", "L0_conv_A_log",
        "L0_conv_dt_bias", "L0_conv_Dp", "L0_conv_norm_w", "L0_conv_W_out", "L0_conv_se_w1", "L0_conv_se_b1",
        "L0_conv_se_w2", "L0_conv_se_b2", "L0_conv_proj_w", "L0_conv_gn_gamma", "L0_conv_gn_beta"]


def kernel(**inputs):
    import concourse.bacc as _bacc
    from concourse.bass_utils import run_bass_kernel_spmd as _run

    nc = _bacc.Bacc("TRN2", target_bir_lowering=False, num_devices=1)
    arrays, aps = {}, {}
    for name in _INS:
        arr = np.ascontiguousarray(inputs[name])
        arrays[f"in_{name}_dram"] = arr
        aps[name.replace("L0_conv_", "")] = nc.dram_tensor(
            f"in_{name}_dram", arr.shape, mybir.dt.from_np(arr.dtype), kind="ExternalInput").ap()
    arrays["shape_const_dram"] = shape_constants()
    aps["shape_const"] = nc.dram_tensor("shape_const_dram", (128, C_COLS), F32, kind="ExternalInput").ap()
    out = nc.dram_tensor("out_0_dram", (BATCH, CH, HEIGHT, WIDTH), F32, kind="ExternalOutput").ap()
    build(nc, aps, out)
    r = _run(nc, [arrays], core_ids=[0])
    return r.results[0]["out_0_dram"]
```
